# Optimizing a Trainium2 kernel written in Bass

```python
import numpy as np
import jax
import jax.numpy as jnp

def _softmax(x, axis=-1):
    return jax.nn.softmax(x, axis=axis)

def _gelu(x):
    return jax.nn.gelu(x, approximate=True)

def _silu(x):
    return jax.nn.silu(x)

def _sigmoid(x):
    return jax.nn.sigmoid(x)

def _layernorm(x, axis=-1, eps=1e-05):
    m = jnp.mean(x, axis=axis, keepdims=True)
    v = jnp.var(x, axis=axis, keepdims=True)
    return (x - m) / jnp.sqrt(v + eps)

def _scatter_add(tgt, idx, src, axis=0):
    return tgt.at[idx].add(src)

def _segment_sum(src, seg, n):
    return jax.ops.segment_sum(src, seg, n)
kernel_name = 'mk_macaron_d1_jaxref_r8_27e66d'

def setup_inputs(seed: int=0):
    np.random.seed(seed)
    _w = jnp.asarray

    def _L0_attn_setup():
        import jax, jax.numpy as jnp
        import numpy as np
        NUM_HEADS = 16
        EPS = 1e-06

        def elu_plus_one(x):
            return jax.nn.elu(x) + 1.0

        def _retrieve(q, memories, memory_norms):
            sigma_q = elu_plus_one(q)
            a_mem = jnp.einsum('bsd,mde->mbse', sigma_q, memories)
            raw = jnp.einsum('bsd,md->mbs', sigma_q, memory_norms)
            per_mem = a_mem / jnp.clip(raw, EPS, None)[..., None]
            rel = raw.mean(axis=-1)
            w = jax.nn.softmax(rel, axis=0)
            return jnp.einsum('mbse,mb->bse', per_mem, w)

        def _local_causal_attention(q, k, v):
            B, S, D = q.shape
            hd = D // NUM_HEADS
            qh = q.reshape(B, S, NUM_HEADS, hd).transpose(0, 2, 1, 3)
            kh = k.reshape(B, S, NUM_HEADS, hd).transpose(0, 2, 1, 3)
            vh = v.reshape(B, S, NUM_HEADS, hd).transpose(0, 2, 1, 3)
            scores = jnp.einsum('bhqd,bhkd->bhqk', qh, kh) * hd ** (-0.5)
            causal = jnp.tril(jnp.ones((S, S), dtype=bool))
            scores = jnp.where(causal, scores, jnp.float32(-1000000000.0))
            attn = jax.nn.softmax(scores, axis=-1)
            out = jnp.einsum('bhqk,bhkd->bhqd', attn, vh)
            return out.transpose(0, 2, 1, 3).reshape(B, S, D)
        key = jax.random.key(seed)
        ks = jax.random.split(key, 8)
        B, S, H, D, M = (2, 256, 256, 256, 4)
        x = jax.random.normal(ks[0], (B, S, H), jnp.float32)
        w_q = jax.random.normal(ks[1], (D, H), jnp.float32) * 0.02
        w_k = jax.random.normal(ks[2], (D, H), jnp.float32) * 0.02
        w_v = jax.random.normal(ks[3], (D, H), jnp.float32) * 0.02
        w_o = jax.random.normal(ks[4], (H, D), jnp.float32) * 0.02
        gate = jnp.zeros((1,), jnp.float32)
        memories = jax.random.normal(ks[5], (M, D, D), jnp.float32) * 0.02
        memory_norms = jax.random.uniform(ks[6], (M, D), jnp.float32) * float(S)
        return {'x': x, 'w_q': w_q, 'w_k': w_k, 'w_v': w_v, 'w_o': w_o, 'gate': gate, 'memories': memories, 'memory_norms': memory_norms}
    _L0_attn_in = _L0_attn_setup()

    def _L0_ffn_setup():
        import jax, jax.numpy as jnp
        import numpy as np
        TOPK = 6
        CAP = 128
        ROUTE_SCALE = 1.0
        key = jax.random.key(seed)
        k = jax.random.split(key, 6)
        B, T, C = (2, 256, 256)
        E, H, HS = (64, 32, 64)
        std = 0.01
        return {'x': jax.random.normal(k[0], (B, T, C), jnp.float32), 'w_gate': jax.random.normal(k[1], (C, E), jnp.float32) * std, 'w_shared_up': jax.random.normal(k[2], (C, 2 * HS), jnp.float32) * std, 'w_shared_down': jax.random.normal(k[3], (HS, C), jnp.float32) * std, 'w_up': jax.random.normal(k[4], (E, C, 2 * H), jnp.float32) * std, 'w_down': jax.random.normal(k[5], (E, H, C), jnp.float32) * std}
    _L0_ffn_in = _L0_ffn_setup()
    _d = {'L0_attn_x': _L0_attn_in['x'], 'L0_attn_w_q': _L0_attn_in['w_q'], 'L0_attn_w_k': _L0_attn_in['w_k'], 'L0_attn_w_v': _L0_attn_in['w_v'], 'L0_attn_w_o': _L0_attn_in['w_o'], 'L0_attn_gate': _L0_attn_in['gate'], 'L0_attn_memories': _L0_attn_in['memories'], 'L0_attn_memory_norms': _L0_attn_in['memory_norms'], 'L0_ffn_w_gate': _L0_ffn_in['w_gate'], 'L0_ffn_w_shared_up': _L0_ffn_in['w_shared_up'], 'L0_ffn_w_shared_down': _L0_ffn_in['w_shared_down'], 'L0_ffn_w_up': _L0_ffn_in['w_up'], 'L0_ffn_w_down': _L0_ffn_in['w_down']}
    _x0 = _d['L0_attn_x']
    _d['L0_attn_x'] = jax.random.normal(jax.random.fold_in(jax.random.key(seed), 1), (8, 256, 256), dtype=_x0.dtype)
    del _x0
    return _d

def reference(L0_attn_x, L0_attn_w_q, L0_attn_w_k, L0_attn_w_v, L0_attn_w_o, L0_attn_gate, L0_attn_memories, L0_attn_memory_norms, L0_ffn_w_gate, L0_ffn_w_shared_up, L0_ffn_w_shared_down, L0_ffn_w_up, L0_ffn_w_down):

    def _L0_attn_ref(x, w_q, w_k, w_v, w_o, gate, memories, memory_norms):
        import jax, jax.numpy as jnp
        import numpy as np
        NUM_HEADS = 16
        EPS = 1e-06

        def elu_plus_one(x):
            return jax.nn.elu(x) + 1.0

        def _retrieve(q, memories, memory_norms):
            sigma_q = elu_plus_one(q)
            a_mem = jnp.einsum('bsd,mde->mbse', sigma_q, memories)
            raw = jnp.einsum('bsd,md->mbs', sigma_q, memory_norms)
            per_mem = a_mem / jnp.clip(raw, EPS, None)[..., None]
            rel = raw.mean(axis=-1)
            w = jax.nn.softmax(rel, axis=0)
            return jnp.einsum('mbse,mb->bse', per_mem, w)

        def _local_causal_attention(q, k, v):
            B, S, D = q.shape
            hd = D // NUM_HEADS
            qh = q.reshape(B, S, NUM_HEADS, hd).transpose(0, 2, 1, 3)
            kh = k.reshape(B, S, NUM_HEADS, hd).transpose(0, 2, 1, 3)
            vh = v.reshape(B, S, NUM_HEADS, hd).transpose(0, 2, 1, 3)
            scores = jnp.einsum('bhqd,bhkd->bhqk', qh, kh) * hd ** (-0.5)
            causal = jnp.tril(jnp.ones((S, S), dtype=bool))
            scores = jnp.where(causal, scores, jnp.float32(-1000000000.0))
            attn = jax.nn.softmax(scores, axis=-1)
            out = jnp.einsum('bhqk,bhkd->bhqd', attn, vh)
            return out.transpose(0, 2, 1, 3).reshape(B, S, D)
        q = x @ w_q.T
        k = x @ w_k.T
        v = x @ w_v.T
        mem_out = _retrieve(q, memories, memory_norms)
        local_out = _local_causal_attention(q, k, v)
        g = jax.nn.sigmoid(gate)
        out = g * mem_out + (1.0 - g) * local_out
        return out @ w_o.T

    def _L0_ffn_ref(x, w_gate, w_shared_up, w_shared_down, w_up, w_down):
        import jax, jax.numpy as jnp
        import numpy as np
        TOPK = 6
        CAP = 128
        ROUTE_SCALE = 1.0
        B, T, C = x.shape
        E = w_gate.shape[1]
        x_flat = x.reshape(-1, C)
        N = x_flat.shape[0]
        su = x_flat @ w_shared_up
        y_s, g_s = jnp.split(su, 2, axis=-1)
        shared = jax.nn.silu(g_s) * y_s @ w_shared_down
        scores = jax.nn.sigmoid(x_flat @ w_gate)
        _, topk_idx = jax.lax.top_k(scores, TOPK)
        w = jnp.take_along_axis(scores, topk_idx, axis=-1)
        w = w / w.sum(-1, keepdims=True) * ROUTE_SCALE
        flat_e = topk_idx.reshape(-1)
        oh = jax.nn.one_hot(flat_e, E, dtype=jnp.int32)
        pos = jnp.take_along_axis(jnp.cumsum(oh, axis=0), flat_e[:, None], axis=1)[:, 0] - 1
        valid = pos < CAP
        pos_c = jnp.where(valid, pos, CAP - 1)
        token_ids = jnp.repeat(jnp.arange(N), TOPK)
        x_disp = jnp.zeros((E, CAP, C), x.dtype).at[flat_e, pos].set(x_flat[token_ids], mode='drop')
        up = jnp.einsum('ecd,edh->ech', x_disp, w_up)
        g_r, v_r = jnp.split(up, 2, axis=-1)
        h_r = jax.nn.silu(g_r) * v_r
        out_r = jnp.einsum('ech,ehd->ecd', h_r, w_down)
        y_ts = out_r[flat_e, pos_c]
        y_ts = jnp.where(valid[:, None], y_ts, 0.0)
        routed = (y_ts.reshape(N, TOPK, C) * w[:, :, None]).sum(axis=1)
        return (shared + routed).reshape(B, T, C)
    x = L0_attn_x
    x = x + 0.5 * _L0_ffn_ref(_layernorm(x, axis=-1), L0_ffn_w_gate, L0_ffn_w_shared_up, L0_ffn_w_shared_down, L0_ffn_w_up, L0_ffn_w_down)
    x = x + _L0_attn_ref(_layernorm(x, axis=-1), L0_attn_w_q, L0_attn_w_k, L0_attn_w_v, L0_attn_w_o, L0_attn_gate, L0_attn_memories, L0_attn_memory_norms)
    x = x + 0.5 * _L0_ffn_ref(_layernorm(x, axis=-1), L0_ffn_w_gate, L0_ffn_w_shared_up, L0_ffn_w_shared_down, L0_ffn_w_up, L0_ffn_w_down)
    return x

_drawn_inputs = setup_inputs


def setup_inputs(seed=0):
    import zlib

    import numpy as np

    out = dict(_drawn_inputs(seed))
    spreads = {}
    factors = {'L0_attn_w_q': 8.0,
     'L0_attn_w_k': 8.0,
     'L0_attn_w_v': 7.134,
     'L0_attn_w_o': 7.315,
     'L0_attn_memories': 8.0,
     'L0_attn_memory_norms': 8.0,
     'L0_ffn_w_gate': 8.0,
     'L0_ffn_w_shared_up': 8.0,
     'L0_ffn_w_shared_down': 8.0,
     'L0_ffn_w_up': 8.0,
     'L0_ffn_w_down': 8.0}
    for name, (base, spread) in spreads.items():
        noise = np.random.default_rng([zlib.crc32(name.encode()), seed]).standard_normal(out[name].shape)
        drawn = base * np.exp(spread * noise) if base else spread * noise
        out[name] = jnp.asarray(drawn.astype(out[name].dtype))
    for name, factor in factors.items():
        out[name] = (out[name] * factor).astype(out[name].dtype)
    return out
```

```python
from contextlib import ExitStack, contextmanager

import concourse.bass as bass
from concourse import mybir

F32 = mybir.dt.float32
BF16 = mybir.dt.bfloat16
U32 = mybir.dt.uint32
ALU = mybir.AluOpType
ACT = mybir.ActivationFunctionType
AX = mybir.AxisListType

P = 128
B, T, C = 8, 256, 256
N = B * T
NT = N // P
CC = C // P
E, H, HS = 64, 32, 64
TOPK, CAP = 6, 128
EG = 4
NG = E // EG
ROW = C + E
HALF = NT // 2
KEY0 = 2 * N
DUMP = N + P
LN_EPS = 1e-5
NHEAD = 16
HD = C // NHEAD
MEM = 4
CLIP = 1e-6
UNITS = 12
Q_SLOTS = (0, 0, 1, 1, 0, 2)
K_SLOTS = (0, 1, 0, 1, 2, 0)
STACK = HD * len(Q_SLOTS)


def need(eng, sem, count):
    if not (isinstance(count, int) and count <= 0):
        eng.wait_ge(sem, count)


class Own:

    def __init__(self, eng, sem):
        self.eng, self.sem, self.base, self.n = eng, sem, 0, 0

    def mark(self, ins):
        ins.then_inc(self.sem, 1)
        self.n += 1

    def settle(self):
        self.eng.wait_ge(self.sem, self.base + self.n)

    def link(self, ins):
        self.mark(ins)
        self.settle()

    @contextmanager
    def loop(self, start, end, per):
        total = self.base + self.n
        with self.eng.Fori(start, end) as i:
            self.base, self.n = i * per + (total - start * per), 0
            yield i
            assert self.n == per, (self.n, per)
        self.base, self.n = total + (end - start) * per, 0


def program(nc, x_in, w_tok, w_shared_down, w_up, w_down, w_q, w_k, w_v, w_o, memories, norms, gate, thirds, out, xn_rows, acc, layers=2, attention=True):
    ctx = ExitStack()
    with ctx:
        def sb(name, shape, dt=F32):
            return ctx.enter_context(nc.sbuf_tensor(name, shape, dt))

        def sem(name):
            return ctx.enter_context(nc.semaphore(name))

        bank = [ctx.enter_context(nc.psum_tensor(f"bank{i}", [P, 512], F32)) for i in range(8)]

        ident = sb("ident", [P, P])
        identb = sb("identb", [P, P], BF16)
        keybase = sb("keybase", [P, HALF * P])
        dump_row = sb("dump_row", [P, 1])
        zrow = sb("zrow", [P, ROW])
        minus_half = sb("minus_half", [P, NT])
        wtok = sb("wtok", [P, CC, 2 * HS + E])
        wsd = sb("wsd", [HS, C])
        wup = sb("wup", [P, CC, E, 2 * H])
        wdn = sb("wdn", [P, NG, C])
        X = sb("X", [P, NT, C])
        st = sb("st", [P, NT, 6])
        mean = sb("mean", [P, NT])
        dev = sb("dev", [P, NT])
        ve = sb("ve", [P, NT])
        rstd = sb("rstd", [P, NT])
        xnw = sb("xnw", [P, 2, ROW])
        xT = sb("xT", [P, 2, CC * P])
        en = sb("en", [P, 2, HS + E])
        sg = sb("sg", [P, 2, HS + E + 2])
        sh1 = sb("sh1", [P, HS])
        sh = sb("sh", [P, 2, HS])
        shT = sb("shT", [HS, 2, P])
        top8 = sb("top8", [P, 8])
        rep = sb("rep", [P, E + 2])
        ssum = sb("ssum", [P, 3])
        mask = sb("mask", [P, 2, E], BF16)
        K1 = sb("K1", [P, HALF * P])
        L1 = sb("L1", [P, CAP])
        K2 = sb("K2", [E, 2 * CAP])
        L2 = sb("L2", [E, CAP])
        ikey = sb("ikey", [P, E])
        IDX = sb("IDX", [P, E], U32)
        xg = [sb(f"xg{u}", [P, EG, ROW]) for u in range(2)]
        xdT_both = sb("xdT", [P, 2, CC, EG * P])
        xdT = [xdT_both[:, u] for u in range(2)]
        eg = [sb(f"eg{u}", [P, EG, H]) for u in range(2)]
        hbig = [sb(f"hbig{u}", [P, EG * P]) for u in range(2)]
        hT = [sb(f"hT{u}", [P, EG * P]) for u in range(2)]
        ysb_both = sb("ysb", [P, 2, EG, C])
        ysb = [ysb_both[:, u] for u in range(2)]
        fin = sb("fin", [P, NT, C])

        wq, wk, wv, wo = (sb(n, [P, CC, C]) for n in ("wq", "wk", "wv", "wo"))
        mems = sb("mems", [P, CC, MEM * C])
        nrm = sb("nrm", [P, CC, MEM])
        gt = sb("gt", [P, 4])
        mean_w = sb("mean_w", [P, P])
        causal = sb("causal", [P, 4, P], BF16)
        xn = sb("xn", [P, 2, C])
        xT2 = sb("xT2", [P, CC, T])
        qT = sb("qT", [P, CC * T])
        kT = sb("kT", [P, CC * T])
        rest = [sb(f"rest{w}", [P, CC * T]) for w in range(2)]
        part = [sb(f"part{w}", [P, 3, CC * T], BF16) for w in range(2)]
        def stacks(ap, count):
            flat = ap.bitcast(BF16).rearrange("p (u h t) -> p u h t", u=count, h=NHEAD)
            return [flat[0:STACK, u] for u in range(count)]

        QS = stacks(fin[:].rearrange("p t c -> p (t c)"), 2)
        KS = stacks(ysb_both[:].rearrange("p u e c -> p (u e c)"), 1) + \
            stacks(xdT_both[:].rearrange("p u c s -> p (u c s)"), 1)
        V = [sb(f"V{u}", [P, 2, NHEAD, HD + 1]) for u in range(2)]
        sigma = [sb(f"sigma{u}", [P, CC, T]) for u in range(2)]
        raw = sb("raw", [P, 2, MEM])
        rawc = sb("rawc", [P, 2, MEM])
        rel = sb("rel", [P, MEM])
        wm = sb("wm", [P, 2 * MEM])
        wsc = sb("wsc", [P, 4])
        coef = sb("coef", [P, 2, MEM])
        memo = sb("memo", [P, 2, C])
        negmax = [sb(f"negmax{u}", [P, 4]) for u in range(2)]
        Pr = [sb(f"Pr{u}", [P, 512]) for u in range(2)]
        PT = [sb(f"PT{u}", [P, 512]) for u in range(2)]
        rl = sb("rl", [P, 2, NHEAD])
        mix = sb("mix", [P, 2, C])
        mixT = sb("mixT", [P, CC, T])

        x_loaded, w_loaded = sem("x_loaded"), sem("w_loaded")
        const_set, const_ready = sem("const_set"), sem("const_ready")
        dve_own = sem("dve_own")
        var_ready, rstd_ready = sem("var_ready"), sem("rstd_ready")
        xn_ready, xT_psum, xT_ready, proj_ready, e_ready = (
            sem("xn_ready"), sem("xT_psum"), sem("xT_ready"), sem("proj_ready"), sem("e_ready"))
        sh_ready, mask_ready, wrow_ready = sem("sh_ready"), sem("mask_ready"), sem("wrow_ready")
        maskT_psum, keys_done, shT_psum, shT_ready = (
            sem("maskT_psum"), sem("keys_done"), sem("shT_psum"), sem("shT_ready"))
        shd_psum, x_shared = sem("shd_psum"), sem("x_shared")
        row_stored = [sem("row_stored0"), sem("row_stored1")]
        lists_ready, listsT_psum, idx_ready = (
            sem("lists_ready"), sem("listsT_psum"), sem("idx_ready"))
        gathered = [sem("gathered0"), sem("gathered1")]
        t0_psum, t1_psum, xd0_ready, xd1_ready = (
            sem("t0_psum"), sem("t1_psum"), sem("xd0_ready"), sem("xd1_ready"))
        up_psum, eg_ready, h_ready, hT_psum, hT_ready = (
            sem("up_psum"), sem("eg_ready"), sem("h_ready"), sem("hT_psum"), sem("hT_ready"))
        y_psum, ya_ready, yb_ready = sem("y_psum"), sem("ya_ready"), sem("yb_ready")
        acc_set = [sem("acc_set0"), sem("acc_set1")]
        acc_done = [sem("acc_done0"), sem("acc_done1")]
        fin_loaded = [sem(f"fin_loaded{c}") for c in range(4)]
        summed, stored = sem("summed"), sem("stored")
        aw_loaded, gate_exp, gate_ready = sem("aw_loaded"), sem("gate_exp"), sem("gate_ready")
        xn2_ready, xT2_psum, xT2_ready = sem("xn2_ready"), sem("xT2_psum"), sem("xT2_ready")
        q_psum, q_ready, k_psum, k_ready, v_psum, v_ready = (
            sem("q_psum"), sem("q_ready"), sem("k_psum"), sem("k_ready"), sem("v_psum"), sem("v_ready"))
        expq_ready, sigma_ready = sem("expq_ready"), sem("sigma_ready")
        pool_own = sem("pool_own")
        thirds_ready, thirds_stored = sem("thirds_ready"), sem("thirds_stored")
        stacked = [sem("stacked0"), sem("stacked1")]
        raw_psum, raw_ready, rel_psum, rel_ready, wm_ready = (
            sem("raw_psum"), sem("raw_ready"), sem("rel_psum"), sem("rel_ready"), sem("wm_ready"))
        mem_psum, mem_used = sem("mem_psum"), sem("mem_used")
        s_psum, max_ready, p_ready, pt_psum, pt_ready, pv_done = (
            sem("s_psum"), sem("max_ready"), sem("p_ready"), sem("pt_psum"), sem("pt_ready"), sem("pv_done"))
        mix_ready, mixT_psum, mixT_ready, wo_psum, wo_used = (
            sem("mix_ready"), sem("mixT_psum"), sem("mixT_ready"), sem("wo_psum"), sem("wo_used"))

        ZPARTS = NT // 4 + 1
        INIT = [16 * NT, 16 * ZPARTS]
        ADDS = 16 * E // 2

        def tile_of(i, u):
            return i + HALF * u

        block = ctx.enter_context(nc.Block())

        @block.sync
        def _(sp):
            x_t = x_in.rearrange("(t p) c -> p t c", p=P)
            out_t = out.rearrange("(t p) c -> p t c", p=P)
            rows_t = xn_rows[0:N, :].rearrange("(t p) c -> p t c", p=P)
            acc_t = [a[0:N, :].rearrange("(t p) c -> p t c", p=P) for a in acc]
            sp.dma_start(X[:], x_t).then_inc(x_loaded, 16)
            sp.dma_start(wtok[:], w_tok).then_inc(w_loaded, 16)
            sp.dma_start(wsd[:], w_shared_down).then_inc(w_loaded, 16)
            sp.dma_start(wup[:], w_up).then_inc(w_loaded, 16)
            sp.dma_start(wdn[:], w_down).then_inc(w_loaded, 16)
            for w, src in ((wq, w_q), (wk, w_k), (wv, w_v), (wo, w_o), (mems, memories), (nrm, norms)):
                sp.dma_start(w[:], src).then_inc(aw_loaded, 16)
            sp.dma_start(gt[:, 0:1], gate.to_broadcast([P, 1])).then_inc(aw_loaded, 16)
            sp.wait_ge(const_set, 1)
            for u in range(2):
                sp.dma_start(xn_rows[N + 64 * u:N + 64 * u + 64, :], zrow[64 * u:64 * u + 64, :])\
                  .then_inc(row_stored[u], 16)

            def moe(f):
                if f:
                    sp.wait_ge(fin_loaded[3], 32)
                    for c in range(3):
                        sp.wait_ge(fin_loaded[c], 32)
                zeros = zrow[:, 0:C].rearrange("p (o c) -> p o c", o=1)
                for c in range(ZPARTS):
                    rows = acc[1][4 * P * c:min(4 * P * (c + 1), DUMP), :].rearrange("(t p) c -> p t c", p=P)
                    sp.dma_start(rows, zeros.to_broadcast(list(rows.shape))).then_inc(acc_set[1], 16)
                if not f:
                    sp.dma_start(acc[0][N:DUMP, :], zrow[:, 0:C]).then_inc(w_loaded, 16)

                def store_rows(i, u):
                    s = 2 * i + u + NT * f
                    sp.wait_ge(wrow_ready, s + 1)
                    sp.dma_start(rows_t[:, tile_of(i, u), :], xnw[:, u, :]).then_inc(row_stored[u], 16)

                def store_x(i, u):
                    s = 2 * i + u + NT * f
                    sp.wait_ge(x_shared, s + 1)
                    sp.dma_start(acc_t[0][:, tile_of(i, u), :], X[:, tile_of(i, u), :]).then_inc(acc_set[0], 16)

                store_rows(0, 0)
                with sp.Fori(0, HALF - 1) as i:
                    store_rows(i, 1)
                    store_x(i, 0)
                    store_rows(i + 1, 0)
                    store_x(i, 1)
                store_rows(HALF - 1, 1)
                store_x(HALF - 1, 0)
                store_x(HALF - 1, 1)
                for r in range(2):
                    sp.wait_ge(acc_done[r], ADDS * (f + 1))
                for c in range(4):
                    tiles = slice(4 * c, 4 * c + 4)
                    sp.dma_start(X[:, tiles, :], acc_t[0][:, tiles, :]).then_inc(fin_loaded[c], 16)
                    sp.dma_start(fin[:, tiles, :], acc_t[1][:, tiles, :]).then_inc(fin_loaded[c], 16)

            def stack(b, u):
                for w, (name, slots) in enumerate(((QS, Q_SLOTS), (KS, K_SLOTS))):
                    sp.wait_ge(thirds_ready, 2 * b + w + 1)
                    if u_first(b):
                        pass
                    else:
                        sp.wait_ge(stacked[u], (b - u) * (8 * 2 * len(Q_SLOTS)))
                    for k in range(3):
                        sp.dma_start(thirds[u, w, k].rearrange("(c p) t -> p c t", p=P),
                                     part[w][:, k, :].rearrange("p (c t) -> p c t", c=CC)).then_inc(thirds_stored, 16)
                    sp.wait_ge(thirds_stored, (2 * b + w + 1) * 48)
                    if not u_first(b):
                        sp.wait_ge(s_psum, (b - 1) * UNITS)
                    for s_, k in enumerate(slots):
                        sp.dma_start(name[u][HD * s_:HD * s_ + HD, :, :],
                                     thirds[u, w, k].rearrange("(h d) t -> d h t", d=HD)).then_inc(stacked[u], 16)

            def u_first(b):
                return isinstance(b, int) and b < 2

            def attention_():
                for b in range(B):
                    stack(b, b % 2)

            for f in range(layers):
                moe(f)
                if attention and f == 0:
                    attention_()
            for c in range(4):
                sp.wait_ge(summed, NT * (layers - 1) + 4 * c + 4)
                tiles = slice(4 * c, 4 * c + 4)
                sp.dma_start(out_t[:, tiles, :], X[:, tiles, :]).then_inc(stored, 16)
            sp.wait_ge(stored, 64)

        @block.gpsimd
        def _(pool):
            g = nc.gpsimd
            g.memset(zrow[:], 0.0).then_inc(const_set, 1)
            g.memset(causal[:], 0.0).then_inc(pool_own, 1)
            g.memset(mean_w[:], 1.0 / T).then_inc(const_ready, 1)
            for u in range(2):
                g.memset(V[u][:], 1.0).then_inc(const_ready, 1)
            for m in (ident, identb, hbig[0], hbig[1]):
                g.memset(m[:], 0.0).then_inc(const_set, 1)
            g.memset(minus_half[:], -0.5).then_inc(const_set, 1)
            g.iota(keybase[:], [[-1, HALF * P]], base=KEY0, channel_multiplier=0,
                   allow_small_or_imprecise_dtypes=True).then_inc(const_set, 1)
            g.iota(dump_row[:], [[0, 1]], base=N, channel_multiplier=1,
                   allow_small_or_imprecise_dtypes=True).then_inc(const_set, 1)
            pool.wait_ge(const_set, 8)
            for m in (ident, identb):
                g.affine_select(out=m[:], in_=m[:], compare_op=ALU.not_equal, fill=1.0, base=0,
                                pattern=[[-1, P]], channel_multiplier=1).then_inc(const_ready, 1)
            pool.wait_ge(pool_own, 1)
            g.affine_select(out=causal[:], in_=causal[:], compare_op=ALU.is_ge, fill=-1e9, base=0,
                            pattern=[[0, 4], [-1, P]], channel_multiplier=1).then_inc(const_ready, 1)

            def moe(f):
                pool.wait_ge(var_ready, 2 * f + 1)
                g.tensor_tensor(rstd[:], ve[:], minus_half[:], ALU.pow).then_inc(rstd_ready, 1)
                pool.wait_ge(idx_ready, f + 1)
                for u in range(2):
                    pool.wait_ge(row_stored[u], 16 * (1 + HALF * (f + 1)))
                for r in range(2):
                    pool.wait_ge(acc_set[r], INIT[r] * (f + 1))

                def gather(gi, e):
                    g.indirect_dma_start(out=xg[gi % 2][:, e, :], out_offset=None, in_=xn_rows[:, :],
                                         in_offset=bass.IndirectOffsetOnAxis(IDX[:, EG * gi + e:EG * gi + e + 1], 0))\
                     .then_inc(gathered[gi % 2], 16)

                def scatter(gi, e):
                    r = e % 2
                    if e == 0:
                        pool.wait_ge(ya_ready, gi + NG * f + 1)
                    if e == 2:
                        pool.wait_ge(yb_ready, gi + NG * f + 1)
                    if 2 * gi + e // 2 > 0:
                        pool.wait_ge(acc_done[r], (2 * gi + e // 2) * 16 + ADDS * f)
                    g.indirect_dma_start(out=acc[r][:, :],
                                         out_offset=bass.IndirectOffsetOnAxis(IDX[:, EG * gi + e:EG * gi + e + 1], 0),
                                         in_=ysb[gi % 2][:, e, :], in_offset=None, compute_op=ALU.add)\
                     .then_inc(acc_done[r], 16)

                for gi in range(NG + 2):
                    if 2 <= gi < NG:
                        pool.wait_ge(h_ready, gi - 1 + NG * f)
                    for e in range(EG):
                        if gi < NG:
                            gather(gi, e)
                        if gi >= 2:
                            scatter(gi - 2, e)

            def thirds_of(src, ready, w, b):
                pool.wait_ge(ready, b + 1)
                if not (isinstance(b, int) and b == 0):
                    pool.wait_ge(thirds_stored, b * 96 - 48 + 48 * w)
                base = 1 + 8 * b + 4 * w
                g.tensor_copy(part[w][:, 0, :], src[:]).then_inc(pool_own, 1)
                pool.wait_ge(pool_own, base + 1)
                g.tensor_tensor(rest[w][:], src[:], part[w][:, 0, :], ALU.subtract).then_inc(pool_own, 1)
                pool.wait_ge(pool_own, base + 2)
                g.tensor_copy(part[w][:, 1, :], rest[w][:]).then_inc(pool_own, 1)
                pool.wait_ge(pool_own, base + 3)
                g.tensor_tensor(rest[w][:], rest[w][:], part[w][:, 1, :], ALU.subtract).then_inc(pool_own, 1)
                pool.wait_ge(pool_own, base + 4)
                g.tensor_copy(part[w][:, 2, :], rest[w][:]).then_inc(thirds_ready, 1)

            def attention_():
                pool.wait_ge(var_ready, 2)
                g.tensor_tensor(rstd[:], ve[:], minus_half[:], ALU.pow).then_inc(rstd_ready, 1)
                for b in range(B):
                    thirds_of(qT, q_ready, 0, b)
                    thirds_of(kT, k_ready, 1, b)

            for f in range(layers):
                moe(f)
                if attention and f == 0:
                    attention_()

        @block.scalar
        def _(act):
            a = nc.scalar

            def moe(f):
                def copy_xT(i, u):
                    s = 2 * i + u + NT * f
                    act.wait_ge(xT_psum, s + 1)
                    a.activation(xT[:, u, :], bank[u][:, 0:CC * P], ACT.Copy).then_inc(xT_ready, 1)

                def exp_gates(i, u):
                    s = 2 * i + u + NT * f
                    act.wait_ge(proj_ready, s + 1)
                    a.activation(en[:, u, :], bank[2 + u][:, HS:2 * HS + E], ACT.Exp, scale=-1.0).then_inc(e_ready, 1)

                def copy_shT(i, u):
                    s = 2 * i + u + NT * f
                    act.wait_ge(shT_psum, s + 1)
                    a.activation(shT[:, u, :], bank[5][0:HS, 0:P], ACT.Copy).then_inc(shT_ready, 1)

                def step(i, u, last=False):
                    if not last:
                        copy_xT(i + u, 1 - u)
                        exp_gates(i + u, 1 - u)
                    copy_shT(i, u)

                copy_xT(0, 0)
                exp_gates(0, 0)
                with act.Fori(0, HALF - 1) as i:
                    step(i, 0)
                    step(i, 1)
                step(HALF - 1, 0)
                step(HALF - 1, 1, last=True)

                def copy_xd(i, u):
                    act.wait_ge(t0_psum, 2 * i + u + NG * f + 1)
                    a.activation(xdT[u][:, 0, :], bank[0][:], ACT.Copy).then_inc(xd0_ready, 1)

                def copy_hT(i, u):
                    act.wait_ge(hT_psum, 2 * i + u + NG * f + 1)
                    a.activation(hT[u][:], bank[4][:], ACT.Copy).then_inc(hT_ready, 1)

                def exp_up(i, u):
                    act.wait_ge(up_psum, 2 * i + u + NG * f + 1)
                    v = bank[2 + u][:, 0:EG * 2 * H].rearrange("p (e h) -> p e h", e=EG)
                    a.activation(eg[u][:], v[:, :, 0:H], ACT.Exp, scale=-1.0).then_inc(eg_ready, 1)

                def copy_y(i, u):
                    act.wait_ge(y_psum, 2 * i + u + NG * f + 1)
                    if not (isinstance(i, int) and i == 0):
                        act.wait_ge(acc_done[0], i * 64 + (32 * u - 48 + ADDS * f))
                        act.wait_ge(acc_done[1], i * 64 + (32 * u - 48 + ADDS * f))
                    a.activation(ysb[u][:, 0:2, :], bank[5][:].rearrange("p (e c) -> p e c", e=2), ACT.Copy)\
                     .then_inc(ya_ready, 1)

                def estep(i, u, last=False):
                    if not last:
                        copy_xd(i + u, 1 - u)
                    copy_hT(i, u)
                    if not last:
                        exp_up(i + u, 1 - u)
                    copy_y(i, u)

                copy_xd(0, 0)
                exp_up(0, 0)
                estep(0, 0)
                estep(0, 1)
                with act.Fori(1, NG // 2 - 1) as i:
                    estep(i, 0)
                    estep(i, 1)
                estep(NG // 2 - 1, 0)
                estep(NG // 2 - 1, 1, last=True)

            def exps(b, u, n):
                U = UNITS * b + n
                need(act, max_ready, U + 1)
                need(act, pt_psum, U - 1)
                k = 4 if n % 3 == 0 else 2
                w = 512 // k
                for i in range(k):
                    last = a.activation(Pr[n % 2][:, w * i:w * i + w], bank[n % 2][:, w * i:w * i + w], ACT.Exp,
                                        bias=negmax[n % 2][:, i:i + 1])
                last.then_inc(p_ready, 1)

            def copy_qT(b, u):
                act.wait_ge(q_psum, b + 1)
                need(act, thirds_ready, 2 * b - 1)
                need(act, sigma_ready, b)
                a.activation(qT[:], bank[6][:], ACT.Copy).then_inc(q_ready, 1)
                act.wait_ge(q_ready, b + 1)
                a.activation(sigma[u][:].rearrange("p c t -> p (c t)"), qT[:], ACT.Exp).then_inc(expq_ready, 1)

            def copy_kT(b):
                act.wait_ge(k_psum, b + 1)
                need(act, thirds_ready, 2 * b)
                a.activation(kT[:], bank[6][:], ACT.Copy, scale=HD ** -0.5).then_inc(k_ready, 1)

            def copy_xT2(b):
                act.wait_ge(xT2_psum, b + 1)
                a.activation(xT2[:].rearrange("p c t -> p (c t)"), bank[7][:], ACT.Copy).then_inc(xT2_ready, 1)

            def copy_v(b, u):
                act.wait_ge(v_psum, b + 1)
                a.activation(V[u][:, :, :, 0:HD], bank[6][:].rearrange("p (t h d) -> p t h d", t=2, h=NHEAD), ACT.Copy)\
                 .then_inc(v_ready, 1)

            def body(b, u, first=False, last=False):
                for n in range(UNITS):
                    if n == 1 and not last:
                        copy_xT2(b + 1)
                    if n == 2:
                        act.wait_ge(rel_ready, b + 1)
                        a.activation(wm[:, 0:MEM], rel[:], ACT.Exp, bias=wsc[:, 0:1], accum_out=wsc[:, 1:2])\
                         .then_inc(wm_ready, 1)
                        if not last:
                            copy_qT(b + 1, 1 - u)
                    if n == 3 and not first:
                        act.wait_ge(mixT_psum, b)
                        a.activation(mixT[:].rearrange("p c t -> p (c t)"), bank[7][:], ACT.Copy).then_inc(mixT_ready, 1)
                    if n == 4 and not last:
                        copy_kT(b + 1)
                    if n == 6 and not last:
                        copy_v(b + 1, 1 - u)
                    exps(b, u, n)

            def attention_():
                act.wait_ge(aw_loaded, 112)
                a.activation(gt[:, 1:2], gt[:, 0:1], ACT.Exp, scale=-1.0).then_inc(gate_exp, 1)
                copy_xT2(0)
                copy_qT(0, 0)
                copy_kT(0)
                copy_v(0, 0)
                body(0, 0, first=True)
                with act.Fori(0, B // 2 - 1) as i:
                    body(2 * i + 1, 1)
                    body(2 * i + 2, 0)
                body(B - 1, 1, last=True)
                act.wait_ge(mixT_psum, B)
                a.activation(mixT[:].rearrange("p c t -> p (c t)"), bank[7][:], ACT.Copy).then_inc(mixT_ready, 1)

            for f in range(layers):
                moe(f)
                if attention and f == 0:
                    attention_()

        @block.vector
        def _(dve):
            v = nc.vector
            own = Own(dve, dve_own)

            def stats(t):
                own.mark(v.bn_stats(st[:, t, :], X[:, t, :]))

            def variance():
                own.settle()
                own.mark(v.tensor_tensor(mean[:], st[:, :, 1], st[:, :, 4], ALU.add))
                own.mark(v.tensor_tensor(dev[:], st[:, :, 1], st[:, :, 4], ALU.subtract))
                own.link(v.tensor_tensor(ve[:], st[:, :, 2], st[:, :, 5], ALU.add))
                own.mark(v.tensor_scalar(mean[:], mean[:], 0.5, None, ALU.mult))
                own.mark(v.tensor_scalar(ve[:], ve[:], 1.0 / C, LN_EPS, ALU.mult, ALU.add))
                own.link(v.scalar_tensor_tensor(dev[:], dev[:], 0.25, dev[:], ALU.mult, ALU.mult))
                v.tensor_tensor(ve[:], ve[:], dev[:], ALU.add).then_inc(var_ready, 1)

            own.mark(v.memset(sg[:, 0, HS + E:], -1.0))
            own.mark(v.memset(sg[:, 1, HS + E:], -1.0))
            dve.wait_ge(const_set, 8)
            own.mark(v.tensor_scalar_add(keybase[E:P, :], keybase[E:P, :], -float(HALF * P)))
            dve.wait_ge(x_loaded, 16)
            with own.loop(0, NT, 1) as t:
                stats(t)
            variance()

            def moe(f):
                dve.wait_ge(rstd_ready, 2 * f + 1 if attention else f + 1)

                def normalise(i, u):
                    s = 2 * i + u + NT * f
                    t = tile_of(i, u)
                    dve.wait_ge(row_stored[u], 16 * (1 + HALF * f) + i * 16)
                    v.tensor_scalar(xnw[:, u, 0:C], X[:, t, :], mean[:, bass.ds(t, 1)], rstd[:, bass.ds(t, 1)],
                                    ALU.subtract, ALU.mult).then_inc(xn_ready, 1)

                def route(i, u):
                    s = 2 * i + u + NT * f
                    proj = bank[2 + u]
                    dve.wait_ge(e_ready, s + 1)
                    own.link(v.tensor_scalar_add(sg[:, u, 0:HS + E], en[:, u, :], 1.0))
                    own.link(v.reciprocal(sg[:, u, 0:HS + E], sg[:, u, 0:HS + E]))
                    own.mark(v.tensor_tensor(sh1[:], proj[:, HS:2 * HS], sg[:, u, 0:HS], ALU.mult))
                    own.link(v.max(top8[:], sg[:, u, HS:HS + E]))
                    v.tensor_tensor(sh[:, u, :], proj[:, 0:HS], sh1[:], ALU.mult).then_inc(sh_ready, 1)
                    own.mark(v.reduce_sum(ssum[:, 0:1], top8[:, 0:TOPK], AX.X))
                    own.link(v.memset(top8[:, TOPK:8], -1.0))
                    own.mark(v.reciprocal(ssum[:, 1:2], ssum[:, 0:1]))
                    own.link(v.match_replace(rep[:], top8[:], sg[:, u, HS:], -1.0))
                    v.tensor_tensor(mask[:, u, :], rep[:, 0:E], sg[:, u, HS:HS + E], ALU.is_lt).then_inc(mask_ready, 1)
                    own.link(v.tensor_scalar(ssum[:, 2:3], ssum[:, 1:2], 0.5, None, ALU.mult))
                    dve.wait_ge(mask_ready, s + 1)
                    v.scalar_tensor_tensor(xnw[:, u, C:ROW], sg[:, u, HS:HS + E], ssum[:, 2:3], mask[:, u, :],
                                           ALU.mult, ALU.mult).then_inc(wrow_ready, 1)

                def collect(i, u):
                    s = 2 * i + u + NT * f
                    t = tile_of(i, u)
                    q = slice(64 * u, 64 * u + 64)
                    dve.wait_ge(maskT_psum, s + 1)
                    v.tensor_tensor(K1[q, bass.ds(P * i, P)], bank[4][q, 0:P], keybase[q, bass.ds(P * i, P)], ALU.mult)\
                     .then_inc(keys_done, 1)
                    dve.wait_ge(shd_psum, s + 1)
                    v.scalar_tensor_tensor(X[:, t, :], bank[6 + u][:, 0:C], 0.5, X[:, t, :], ALU.mult, ALU.add)\
                     .then_inc(x_shared, 1)

                normalise(0, 0)
                normalise(0, 1)
                route(0, 0)
                with own.loop(0, HALF - 1, 18) as i:
                    normalise(i + 1, 0)
                    route(i, 1)
                    collect(i, 0)
                    normalise(i + 1, 1)
                    route(i + 1, 0)
                    collect(i, 1)
                route(HALF - 1, 1)
                collect(HALF - 1, 0)
                collect(HALF - 1, 1)

                dve.wait_ge(keys_done, NT * (f + 1))
                def top_keys(lists, keys):
                    for r in range(CAP // 8):
                        own.link(v.max(lists[:, 8 * r:8 * r + 8], keys[:]))
                        own.link(v.match_replace(keys[:], lists[:, 8 * r:8 * r + 8], keys[:], 0.0))

                top_keys(L1, K1)
                own.mark(v.tensor_copy(K2[:, 0:CAP], L1[0:E, :]))
                own.link(v.tensor_copy(K2[:, CAP:], L1[E:P, :]))
                top_keys(L2, K2)
                v.tensor_copy(ssum[0:1, 0:1], L2[0:1, 0:1]).then_inc(lists_ready, 1)
                dve.wait_ge(listsT_psum, f + 1)
                own.link(v.tensor_scalar(ikey[:], bank[7][:, 256:256 + E], -1.0, float(KEY0), ALU.mult, ALU.add))
                v.tensor_scalar(IDX[:], ikey[:], dump_row[:, 0:1], None, ALU.min).then_inc(idx_ready, 1)

                def copy_xd(i, u):
                    dve.wait_ge(t1_psum, 2 * i + u + NG * f + 1)
                    v.tensor_copy(xdT[u][:, 1, :], bank[1][:]).then_inc(xd1_ready, 1)

                def hidden(i, u):
                    gi = 2 * i + u
                    up = bank[2 + u][:, 0:EG * 2 * H].rearrange("p (e h) -> p e h", e=EG)
                    dve.wait_ge(eg_ready, gi + NG * f + 1)
                    own.link(v.tensor_scalar_add(eg[u][:], eg[u][:], 1.0))
                    own.link(v.reciprocal(eg[u][:], eg[u][:]))
                    own.link(v.tensor_tensor(eg[u][:], up[:, :, 0:H], eg[u][:], ALU.mult))
                    own.link(v.tensor_tensor(eg[u][:], up[:, :, H:], eg[u][:], ALU.mult))
                    w = xg[u][:].rearrange("p e c -> p (e c)")[:, bass.ds(EG * gi + C, EG, ROW + 1)]
                    w = w.rearrange("p (e o) -> p e o", o=1).to_broadcast([P, EG, H])
                    diag = hbig[u][:].rearrange("p (e q) -> p e q", e=EG)
                    for e in range(EG):
                        last = v.tensor_scalar(hbig[u][:, e * P + e * H:e * P + e * H + H], eg[u][:, e, :],
                                               xg[u][:, e, bass.ds(EG * gi + C + e, 1)], None, ALU.mult)
                        if e < EG - 1:
                            own.mark(last)
                    last.then_inc(h_ready, 1)

                def copy_y(i, u):
                    dve.wait_ge(y_psum, 2 * i + u + NG * f + 1)
                    if not (isinstance(i, int) and i == 0):
                        dve.wait_ge(acc_done[0], i * 64 + (32 * u - 32 + ADDS * f))
                        dve.wait_ge(acc_done[1], i * 64 + (32 * u - 32 + ADDS * f))
                    v.tensor_copy(ysb[u][:, 2:4, :], bank[6][:].rearrange("p (e c) -> p e c", e=2)).then_inc(yb_ready, 1)

                def estep(i, u, last=False):
                    if not last:
                        copy_xd(i + u, 1 - u)
                        hidden(i + u, 1 - u)
                    copy_y(i, u)

                copy_xd(0, 0)
                hidden(0, 0)
                estep(0, 0)
                estep(0, 1)
                with own.loop(1, NG // 2 - 1, 14) as i:
                    estep(i, 0)
                    estep(i, 1)
                estep(NG // 2 - 1, 0)
                estep(NG // 2 - 1, 1, last=True)

                for c in range(4):
                    dve.wait_ge(fin_loaded[c], 32 * (f + 1))
                    with own.loop(4 * c, 4 * c + 4, 1 if f + 1 < layers else 0) as t:
                        v.tensor_tensor(X[:, t, :], X[:, t, :], fin[:, t, :], ALU.add).then_inc(summed, 1)
                        if f + 1 < layers:
                            dve.wait_ge(summed, NT * f + t + 1)
                            stats(t)
                if f + 1 < layers:
                    variance()

            def rowmax(b, n):
                U = UNITS * b + n
                k = 4 if n % 3 == 0 else 2
                dve.wait_ge(s_psum, U + 1)
                v.tensor_reduce(negmax[n % 2][:, 0:k], bank[n % 2][:].rearrange("p (h t) -> p h t", h=k), AX.X, ALU.max,
                                negate=True).then_inc(max_ready, 1)

            def copy_pt(U, n):
                dve.wait_ge(pt_psum, U + 1)
                need(dve, pv_done, U - 1)
                v.tensor_copy(PT[n % 2][:], bank[2 + n % 2][:]).then_inc(pt_ready, 1)

            def normalise2(b):
                for t in range(2):
                    last = v.tensor_scalar(xn[:, t, :], X[:, 2 * b + t, :], mean[:, bass.ds(2 * b + t, 1)],
                                           rstd[:, bass.ds(2 * b + t, 1)], ALU.subtract, ALU.mult)
                    last.then_inc(xn2_ready, 1)

            def sigmas(b, u):
                flat = sigma[u][:].rearrange("p c t -> p (c t)")
                dve.wait_ge(expq_ready, b + 1)
                own.link(v.tensor_scalar(flat, flat, 1.0, None, ALU.min))
                v.scalar_tensor_tensor(flat, qT[:], 0.0, flat, ALU.max, ALU.add).then_inc(sigma_ready, 1)

            def raws(b):
                dve.wait_ge(raw_psum, b + 1)
                v.tensor_copy(raw[:].rearrange("p t m -> p (t m)"), bank[6][:, 0:2 * MEM]).then_inc(raw_ready, 1)

            def rels(b):
                dve.wait_ge(rel_psum, b + 1)
                own.link(v.tensor_copy(rel[:], bank[6][:, 16:16 + MEM]))
                v.tensor_reduce(wsc[:, 0:1], rel[:], AX.X, ALU.max, negate=True).then_inc(rel_ready, 1)

            def coefs(b):
                own.link(v.tensor_scalar(rawc[:], raw[:], CLIP, None, ALU.max))
                own.link(v.reciprocal(rawc[:], rawc[:]))
                dve.wait_ge(wm_ready, b + 1)
                own.link(v.reciprocal(wsc[:, 2:3], wsc[:, 1:2]))
                own.link(v.tensor_scalar(wm[:, MEM:], wm[:, 0:MEM], wsc[:, 2:3], gt[:, 2:3], ALU.mult, ALU.mult))
                for t in range(2):
                    own.mark(v.tensor_tensor(coef[:, t, :], rawc[:, t, :], wm[:, MEM:], ALU.mult))

            def mem_sum(b, j):
                t, half = j // 2, j % 2
                if j == 0:
                    own.settle()
                dve.wait_ge(mem_psum, 4 * b + j + 1)
                pm = bank[6 + (7 + j) % 2]
                for k in range(2):
                    src, c = pm[:, C * k:C * k + C], coef[:, t, 2 * half + k:2 * half + k + 1]
                    if half == 0 and k == 0:
                        own.link(v.tensor_scalar(memo[:, t, :], src, c, None, ALU.mult))
                    elif k == 0:
                        own.link(v.scalar_tensor_tensor(memo[:, t, :], src, c, memo[:, t, :], ALU.mult, ALU.add))
                    else:
                        v.scalar_tensor_tensor(memo[:, t, :], src, c, memo[:, t, :], ALU.mult, ALU.add)\
                         .then_inc(mem_used, 1)
                        if half == 0:
                            dve.wait_ge(mem_used, 4 * b + j + 1)

            def finalise(b):
                dve.wait_ge(pv_done, UNITS * b + UNITS)
                o = [bank[4 + t][:, 0:NHEAD * (HD + 1)].rearrange("p (h d) -> p h d", h=NHEAD) for t in range(2)]
                for t in range(2):
                    own.mark(v.reciprocal(rl[:, t, :], o[t][:, :, HD]))
                own.settle()
                own.link(v.tensor_scalar(rl[:], rl[:], gt[:, 3:4], None, ALU.mult))
                for t in range(2):
                    w = rl[:, t, :].rearrange("p (h o) -> p h o", o=1).to_broadcast([P, NHEAD, HD])
                    own.mark(v.tensor_tensor(mix[:, t, :].rearrange("p (h d) -> p h d", h=NHEAD), o[t][:, :, 0:HD], w,
                                             ALU.mult))
                own.settle()
                dve.wait_ge(mem_used, 4 * b + 4)
                v.tensor_tensor(mix[:], mix[:], memo[:], ALU.add).then_inc(mix_ready, 1)

            def residual(b):
                dve.wait_ge(wo_psum, b + 1)
                x2 = X[:, bass.ds(2 * b, 2), :]
                v.tensor_tensor(x2, x2, bank[7][:].rearrange("p (t c) -> p t c", t=2), ALU.add).then_inc(wo_used, 1)
                dve.wait_ge(wo_used, b + 1)
                stats(2 * b)
                stats(2 * b + 1)

            def body(b, u, first=False, last=False):
                for n in range(UNITS):
                    U = UNITS * b + n
                    rowmax(b, n)
                    if n or not first:
                        copy_pt(U - 1, (n - 1) % UNITS)
                    if n == 0:
                        raws(b)
                        if not last:
                            normalise2(b + 1)
                    if n == 1:
                        rels(b)
                    if n == 2 and not first:
                        finalise(b - 1)
                    if n == 3 and not last:
                        sigmas(b + 1, 1 - u)
                    if n == 4:
                        coefs(b)
                    if n == 5 and not first:
                        residual(b - 1)
                    if 7 <= n < 11:
                        mem_sum(b, n - 7)

            def attention_():
                dve.wait_ge(gate_exp, 1)
                own.link(v.tensor_scalar_add(gt[:, 1:2], gt[:, 1:2], 1.0))
                own.link(v.reciprocal(gt[:, 2:3], gt[:, 1:2]))
                own.link(v.tensor_scalar(gt[:, 3:4], gt[:, 2:3], -1.0, 1.0, ALU.mult, ALU.add))
                dve.wait_ge(rstd_ready, 2)
                normalise2(0)
                sigmas(0, 0)
                body(0, 0, first=True)
                with own.loop(0, B // 2 - 1, 2 * 19) as i:
                    body(2 * i + 1, 1)
                    body(2 * i + 2, 0)
                body(B - 1, 1, last=True)
                copy_pt(UNITS * B - 1, UNITS - 1)
                finalise(B - 1)
                residual(B - 1)
                variance()

            for f in range(layers):
                moe(f)
                if attention and f == 0:
                    attention_()

        @block.tensor
        def _(pe):
            m = nc.tensor
            pe.wait_ge(const_ready, 2)
            pe.wait_ge(w_loaded, 80)

            def moe(f):
                def project(i, u):
                    s = 2 * i + u + NT * f
                    pe.wait_ge(xn_ready, s + 1)
                    for c in range(CC):
                        last = m.transpose(bank[u][:, P * c:P * c + P], xnw[:, u, P * c:P * c + P], ident[:])
                    last.then_inc(xT_psum, 1)
                    pe.wait_ge(xT_ready, s + 1)
                    for c in range(CC):
                        last = m.matmul(bank[2 + u][:, 0:2 * HS + E], xT[:, u, P * c:P * c + P], wtok[:, c, :],
                                        start=(c == 0), stop=(c == CC - 1))
                    last.then_inc(proj_ready, 1)

                def turn(i, u):
                    s = 2 * i + u + NT * f
                    q = slice(64 * u, 64 * u + 64)
                    pe.wait_ge(sh_ready, s + 1)
                    pe.wait_ge(mask_ready, s + 1)
                    if f or not isinstance(i, int) or i > 0 or u > 0:
                        pe.wait_ge(keys_done, s)
                    m.matmul(bank[4][q, 0:P], mask[:, u, :], identb[:], start=True, stop=True).then_inc(maskT_psum, 1)
                    m.transpose(bank[5][0:HS, 0:P], sh[:, u, :], ident[:]).then_inc(shT_psum, 1)

                def shared_down(i, u):
                    s = 2 * i + u + NT * f
                    pe.wait_ge(shT_ready, s + 1)
                    m.matmul(bank[6 + u][:, 0:C], shT[:, u, :], wsd[:], start=True, stop=True).then_inc(shd_psum, 1)

                project(0, 0)
                project(0, 1)
                turn(0, 0)
                shared_down(0, 0)
                with pe.Fori(0, HALF - 1) as i:
                    project(i + 1, 0)
                    turn(i, 1)
                    shared_down(i, 1)
                    project(i + 1, 1)
                    turn(i + 1, 0)
                    shared_down(i + 1, 0)
                turn(HALF - 1, 1)
                shared_down(HALF - 1, 1)

                pe.wait_ge(lists_ready, f + 1)
                m.transpose(bank[7][:, 256:256 + E], L2[:], ident[0:E, 0:E]).then_inc(listsT_psum, 1)

                def turn_rows(i, u):
                    gi = 2 * i + u
                    pe.wait_ge(gathered[u], 64 * (NG // 2 * f + 1) + i * 64)
                    for c, sem_ in enumerate((t0_psum, t1_psum)):
                        for e in range(EG):
                            last = m.transpose(bank[c][:, P * e:P * e + P], xg[u][:, e, P * c:P * c + P], ident[:])
                        last.then_inc(sem_, 1)

                def up(i, u):
                    gi = 2 * i + u
                    pe.wait_ge(xd0_ready, gi + NG * f + 1)
                    pe.wait_ge(xd1_ready, gi + NG * f + 1)
                    for e in range(EG):
                        for c in range(CC):
                            last = m.matmul(bank[2 + u][:, 2 * H * e:2 * H * e + 2 * H], xdT[u][:, c, P * e:P * e + P],
                                            wup[:, c, EG * gi + e, :], start=(c == 0), stop=(c == CC - 1))
                    last.then_inc(up_psum, 1)

                def turn_hidden(i, u):
                    pe.wait_ge(h_ready, 2 * i + u + NG * f + 1)
                    for e in range(EG):
                        last = m.transpose(bank[4][:, P * e:P * e + P], hbig[u][:, P * e:P * e + P], ident[:])
                    last.then_inc(hT_psum, 1)

                def down(i, u):
                    gi = 2 * i + u
                    pe.wait_ge(hT_ready, gi + NG * f + 1)
                    if f or not isinstance(i, int) or i > 0 or u > 0:
                        pe.wait_ge(ya_ready, gi + NG * f)
                        pe.wait_ge(yb_ready, gi + NG * f)
                    for e in range(EG):
                        last = m.matmul(bank[5 + e // 2][:, C * (e % 2):C * (e % 2) + C], hT[u][:, P * e:P * e + P],
                                        wdn[:, gi, :], start=True, stop=True)
                    last.then_inc(y_psum, 1)

                def estep(i, u, last=False):
                    if not last:
                        turn_rows(i + u, 1 - u)
                    turn_hidden(i, u)
                    if not last:
                        up(i + u, 1 - u)
                    down(i, u)

                turn_rows(0, 0)
                up(0, 0)
                estep(0, 0)
                with pe.Fori(0, NG // 2 - 1) as i:
                    estep(i, 1)
                    estep(i + 1, 0)
                estep(NG // 2 - 1, 1, last=True)

            def scores(b, u, n):
                U = UNITS * b + n
                if n == 0:
                    pe.wait_ge(stacked[u], (b - u + 2) * (8 * 2 * len(Q_SLOTS)))
                need(pe, p_ready, U - 1)
                hg, j = n // 3, n % 3
                out_, heads = bank[n % 2], range(4 * hg, 4 * hg + 4) if j == 0 else range(4 * hg + 2 * j - 2, 4 * hg + 2 * j)
                q0, w = (0, P) if j == 0 else (P, T)
                for i, h in enumerate(heads):
                    m.matmul(out_[:, w * i:w * i + w], QS[u][:, h, q0:q0 + P], KS[u][:, h, 0:w],
                             start=(i == 0), stop=False, skip_group_check=True)
                diag = out_[:].rearrange("p (h t) -> p h t", t=w)[:, :, w - P:w]
                m.matmul(diag, identb[:], causal[:, 0:len(heads), :], start=False, stop=True,
                         skip_group_check=True).then_inc(s_psum, 1)

            def turn_p(U, n):
                pe.wait_ge(p_ready, U + 1)
                need(pe, pt_ready, U - 1)
                for i in range(4):
                    last = m.transpose(bank[2 + n % 2][:, P * i:P * i + P], Pr[n % 2][:, P * i:P * i + P], ident[:])
                last.then_inc(pt_psum, 1)

            def values(b, u, n):
                U = UNITS * b + n
                pe.wait_ge(pt_ready, U + 1)
                if n == 0:
                    pe.wait_ge(v_ready, b + 1)
                    need(pe, mix_ready, b)
                hg, j = n // 3, n % 3
                for i in range(4):
                    h, t, kb = (4 * hg + i, 0, 0) if j == 0 else (4 * hg + 2 * j - 2 + i // 2, 1, i % 2)
                    last = m.matmul(bank[4 + t][:, (HD + 1) * h:(HD + 1) * h + HD + 1], PT[n % 2][:, P * i:P * i + P],
                                    V[u][:, kb, h, :], start=(kb == 0), stop=(kb == t))
                last.then_inc(pv_done, 1)

            def turn_x(b):
                pe.wait_ge(xn2_ready, 2 * b + 2)
                need(pe, mem_used, 4 * b - 4)
                for c in range(CC):
                    for t in range(2):
                        last = m.transpose(bank[7][:, T * c + P * t:T * c + P * t + P], xn[:, t, P * c:P * c + P], ident[:])
                last.then_inc(xT2_psum, 1)

            def project_t(b, w, done):
                for d in range(CC):
                    for c in range(CC):
                        last = m.matmul(bank[6][:, T * d:T * d + T], w[:, c, P * d:P * d + P], xT2[:, c, :],
                                        start=(c == 0), stop=(c == CC - 1))
                last.then_inc(done, 1)

            def q_job(b):
                pe.wait_ge(xT2_ready, b + 1)
                need(pe, rel_ready, b)
                project_t(b, wq, q_psum)

            def k_job(b):
                pe.wait_ge(q_ready, b + 1)
                project_t(b, wk, k_psum)

            def v_job(b):
                pe.wait_ge(k_ready, b + 1)
                for t in range(2):
                    for c in range(CC):
                        last = m.matmul(bank[6][:, C * t:C * t + C], xT2[:, c, P * t:P * t + P], wv[:, c, :],
                                        start=(c == 0), stop=(c == CC - 1))
                last.then_inc(v_psum, 1)

            def raw_job(b, u):
                pe.wait_ge(sigma_ready, b + 1)
                need(pe, mem_used, 4 * b)
                if isinstance(b, int) and b == 0:
                    pe.wait_ge(v_ready, 1)
                for t in range(2):
                    for c in range(CC):
                        last = m.matmul(bank[6][:, MEM * t:MEM * t + MEM], sigma[u][:, c, P * t:P * t + P], nrm[:, c, :],
                                        start=(c == 0), stop=(c == CC - 1))
                last.then_inc(raw_psum, 1)

            def rel_job(b):
                pe.wait_ge(raw_ready, b + 1)
                for t in range(2):
                    last = m.matmul(bank[6][:, 16:16 + MEM], mean_w[:], raw[:, t, :], start=(t == 0), stop=(t == 1))
                last.then_inc(rel_psum, 1)

            def mem_job(b, u, j, last_batch):
                if j == 0:
                    need(pe, wo_used, b)
                if j == 1:
                    pe.wait_ge(rel_ready, b + 1)
                    pe.wait_ge(v_ready, b + 1 if last_batch else b + 2)
                if j >= 2:
                    pe.wait_ge(mem_used, 4 * b + j - 1)
                for c in range(CC):
                    last = m.matmul(bank[6 + (7 + j) % 2][:], sigma[u][:, c, P * (j // 2):P * (j // 2) + P],
                                    mems[:, c, 512 * (j % 2):512 * (j % 2) + 512], start=(c == 0), stop=(c == CC - 1))
                last.then_inc(mem_psum, 1)

            def mix_job(b, last_batch):
                pe.wait_ge(mix_ready, b + 1)
                if not last_batch:
                    pe.wait_ge(xT2_ready, b + 3)
                for c in range(CC):
                    for t in range(2):
                        last = m.transpose(bank[7][:, T * c + P * t:T * c + P * t + P], mix[:, t, P * c:P * c + P], ident[:])
                last.then_inc(mixT_psum, 1)

            def out_job(b):
                pe.wait_ge(mixT_ready, b + 1)
                for t in range(2):
                    for c in range(CC):
                        last = m.matmul(bank[7][:, C * t:C * t + C], mixT[:, c, P * t:P * t + P], wo[:, c, :],
                                        start=(c == 0), stop=(c == CC - 1))
                last.then_inc(wo_psum, 1)

            def body(b, u, first=False, last=False):
                for n in range(UNITS):
                    U = UNITS * b + n
                    scores(b, u, n)
                    if n == 0:
                        raw_job(b, u)
                    if n == 1:
                        rel_job(b)
                    if not last:
                        {1: turn_x, 2: q_job, 4: k_job, 6: v_job}.get(n, lambda b: None)(b + 1)
                    if n == 3 and not first:
                        mix_job(b - 1, last)
                    if n == 5 and not first:
                        out_job(b - 1)
                    if 7 <= n < 11:
                        mem_job(b, u, n - 7, last)
                    if n or not first:
                        turn_p(U - 1, (n - 1) % UNITS)
                    if n >= 2:
                        values(b, u, n - 2)
                    elif not first:
                        values(b - 1, 1 - u, n + UNITS - 2)

            def attention_():
                pe.wait_ge(aw_loaded, 112)
                pe.wait_ge(const_ready, 6)
                turn_x(0)
                q_job(0)
                k_job(0)
                v_job(0)
                body(0, 0, first=True)
                with pe.Fori(0, B // 2 - 1) as i:
                    body(2 * i + 1, 1)
                    body(2 * i + 2, 0)
                body(B - 1, 1, last=True)
                turn_p(UNITS * B - 1, UNITS - 1)
                values(B - 1, 1, UNITS - 2)
                values(B - 1, 1, UNITS - 1)
                mix_job(B - 1, True)
                out_job(B - 1)

            for f in range(layers):
                moe(f)
                if attention and f == 0:
                    attention_()


def kernel(L0_attn_x, L0_attn_w_q, L0_attn_w_k, L0_attn_w_v, L0_attn_w_o, L0_attn_gate, L0_attn_memories,
           L0_attn_memory_norms, L0_ffn_w_gate, L0_ffn_w_shared_up, L0_ffn_w_shared_down, L0_ffn_w_up, L0_ffn_w_down):
    import numpy as np
    import concourse.bacc as bacc
    from concourse.bass_utils import run_bass_kernel_spmd

    def chunked(w):
        return w.reshape(CC, P, -1).transpose(1, 0, 2)

    arrays = {
        "x": np.asarray(L0_attn_x).reshape(N, C),
        "w_tok": chunked(np.concatenate([np.asarray(L0_ffn_w_shared_up), np.asarray(L0_ffn_w_gate)], axis=1)),
        "w_shared_down": np.asarray(L0_ffn_w_shared_down),
        "w_up": np.asarray(L0_ffn_w_up).reshape(E, CC, P, 2 * H).transpose(2, 1, 0, 3),
        "w_down": np.asarray(L0_ffn_w_down).reshape(NG, P, C).transpose(1, 0, 2),
        "w_q": chunked(np.asarray(L0_attn_w_q).T),
        "w_k": chunked(np.asarray(L0_attn_w_k).T),
        "w_v": chunked(np.asarray(L0_attn_w_v).T),
        "w_o": chunked(np.asarray(L0_attn_w_o).T),
        "memories": chunked(np.asarray(L0_attn_memories).transpose(1, 0, 2).reshape(C, MEM * C)),
        "norms": chunked(np.asarray(L0_attn_memory_norms).T),
        "gate": np.asarray(L0_attn_gate).reshape(1, 1),
    }
    arrays = {k: np.ascontiguousarray(a) for k, a in arrays.items()}
    nc = bacc.Bacc("TRN2", target_bir_lowering=False, num_devices=1)
    args = [nc.dram_tensor(k, a.shape, F32, kind="ExternalInput").ap() for k, a in arrays.items()]
    out = nc.dram_tensor("out", (N, C), F32, kind="ExternalOutput").ap()
    xn_rows = nc.dram_tensor("xn_rows", (DUMP, ROW), F32, kind="Internal").ap()
    acc = [nc.dram_tensor(f"acc{r}", (DUMP, C), F32, kind="Internal").ap() for r in range(2)]
    thirds = nc.dram_tensor("thirds", (2, 2, 3, C, T), BF16, kind="Internal").ap()
    program(nc, *args, thirds, out, xn_rows, acc)
    r = run_bass_kernel_spmd(nc, [arrays], core_ids=[0])
    return r.results[0]["out"].reshape(B, T, C)
```

```python
from contextlib import ExitStack, contextmanager

import concourse.bass as bass
from concourse import mybir

F32 = mybir.dt.float32
BF16 = mybir.dt.bfloat16
U32 = mybir.dt.uint32
ALU = mybir.AluOpType
ACT = mybir.ActivationFunctionType
AX = mybir.AxisListType

P = 128
B, T, C = 8, 256, 256
N = B * T
NT = N // P
CC = C // P
E, H, HS = 64, 32, 64
TOPK, CAP = 6, 128
EG = 4
NG = E // EG
META = E + 1
ROW = C + META
SLOTS = E * CAP
TABLE = SLOTS + TOPK * N
DUMP = N + P
HALF = NT // 2
LN_EPS = 1e-5
NHEAD = 16
HD = C // NHEAD
MEM = 4
CLIP = 1e-6
UNITS = 12
Q_SLOTS = (0, 0, 1, 1, 0, 2)
K_SLOTS = (0, 1, 0, 1, 2, 0)
STACK = HD * len(Q_SLOTS)


def need(eng, sem, count):
    if not (isinstance(count, int) and count <= 0):
        eng.wait_ge(sem, count)


class Own:

    def __init__(self, eng, sem):
        self.eng, self.sem, self.base, self.n = eng, sem, 0, 0

    def mark(self, ins):
        ins.then_inc(self.sem, 1)
        self.n += 1

    def settle(self):
        self.eng.wait_ge(self.sem, self.base + self.n)

    def link(self, ins):
        self.mark(ins)
        self.settle()

    @contextmanager
    def loop(self, start, end, per):
        total = self.base + self.n
        with self.eng.Fori(start, end) as i:
            self.base, self.n = i * per + (total - start * per), 0
            yield i
            assert self.n == per, (self.n, per)
        self.base, self.n = total + (end - start) * per, 0


def program(nc, x_in, w_tok, w_shared_down, w_up, w_down, w_q, w_k, w_v, w_o, memories, norms, gate, thirds, out, table, acc, layers=2, attention=True):
    ctx = ExitStack()
    with ctx:
        def sb(name, shape, dt=F32):
            return ctx.enter_context(nc.sbuf_tensor(name, shape, dt))

        def sem(name):
            return ctx.enter_context(nc.semaphore(name))

        bank = [ctx.enter_context(nc.psum_tensor(f"bank{i}", [P, 512], F32)) for i in range(8)]

        ident = sb("ident", [P, P])
        identb = sb("identb", [P, P], BF16)
        before = sb("before", [P, P], BF16)
        ones = sb("ones", [P, P], BF16)
        expert_no = sb("expert_no", [P, E])
        slot_end = sb("slot_end", [P, E])
        over_row = sb("over_row", [P, NT * TOPK])
        zrow = sb("zrow", [P, ROW])
        minus_half = sb("minus_half", [P, NT])
        wtok = sb("wtok", [P, CC, 2 * HS + E])
        wsd = sb("wsd", [HS, C])
        wup = sb("wup", [P, CC, E, 2 * H])
        wdn = sb("wdn", [P, NG, C])
        X = sb("X", [P, NT, C])
        st = sb("st", [P, NT, 6])
        mean = sb("mean", [P, NT])
        dev = sb("dev", [P, NT])
        ve = sb("ve", [P, NT])
        rstd = sb("rstd", [P, NT])
        rows = sb("rows", [P, NT, ROW])
        xT = sb("xT", [P, 2, CC * P])
        en = sb("en", [P, 2, HS + E])
        sg = sb("sg", [P, 2, HS + E + 2])
        sh1 = sb("sh1", [P, HS])
        sh = sb("sh", [P, 2, HS])
        shT = sb("shT", [HS, 2, P])
        top8 = sb("top8", [P, 8])
        rep = sb("rep", [P, E + 2])
        ssum = sb("ssum", [P, 3])
        mask = sb("mask", [P, 2, E], BF16)
        chosen = sb("chosen", [P, E], BF16)
        end_of = sb("end_of", [P, 2, E])
        fits = sb("fits", [P, E])
        key = sb("key", [P, E])
        key8 = sb("key8", [P, 8])
        over = sb("over", [P, TOPK])
        slot = sb("slot", [P, NT, TOPK], U32)
        IDX = sb("IDX", [P, E], U32)
        xg = [sb(f"xg{u}", [P, EG, ROW]) for u in range(2)]
        meta = [sb(f"meta{u}", [P, EG, META]) for u in range(2)]
        xdT_both = sb("xdT", [P, 2, CC, EG * P])
        xdT = [xdT_both[:, u] for u in range(2)]
        eg = [sb(f"eg{u}", [P, EG, H]) for u in range(2)]
        hbig = [sb(f"hbig{u}", [P, EG * P]) for u in range(2)]
        hT = [sb(f"hT{u}", [P, EG * P]) for u in range(2)]
        ysb_both = sb("ysb", [P, 2, EG, C])
        ysb = [ysb_both[:, u] for u in range(2)]
        fin = rows[:].rearrange("p t c -> p (t c)")[:, 0:NT * C].rearrange("p (t c) -> p t c", c=C)

        wq, wk, wv, wo = (sb(n, [P, CC, C]) for n in ("wq", "wk", "wv", "wo"))
        mems = sb("mems", [P, CC, MEM * C])
        nrm = sb("nrm", [P, CC, MEM])
        gt = sb("gt", [P, 4])
        mean_w = sb("mean_w", [P, P])
        causal = sb("causal", [P, 4, P], BF16)
        xn = sb("xn", [P, 2, C])
        xT2 = sb("xT2", [P, CC, T])
        qT = sb("qT", [P, CC * T])
        kT = sb("kT", [P, CC * T])
        rest = [sb(f"rest{w}", [P, CC * T]) for w in range(2)]
        part = [sb(f"part{w}", [P, 3, CC * T], BF16) for w in range(2)]
        def stacks(ap, count):
            flat = ap.bitcast(BF16).rearrange("p (u h t) -> p u h t", u=count, h=NHEAD)
            return [flat[0:STACK, u] for u in range(count)]

        QS = stacks(rows[:].rearrange("p t c -> p (t c)")[:, 0:NT * C], 2)
        KS = stacks(ysb_both[:].rearrange("p u e c -> p (u e c)"), 1) + \
            stacks(xdT_both[:].rearrange("p u c s -> p (u c s)"), 1)
        V = [sb(f"V{u}", [P, 2, NHEAD, HD + 1]) for u in range(2)]
        sigma = [sb(f"sigma{u}", [P, CC, T]) for u in range(2)]
        raw = sb("raw", [P, 2, MEM])
        rawc = sb("rawc", [P, 2, MEM])
        rel = sb("rel", [P, MEM])
        wm = sb("wm", [P, 2 * MEM])
        wsc = sb("wsc", [P, 4])
        coef = sb("coef", [P, 2, MEM])
        memo = sb("memo", [P, 2, C])
        negmax = [sb(f"negmax{u}", [P, 4]) for u in range(2)]
        Pr = [sb(f"Pr{u}", [P, 512]) for u in range(2)]
        PT = [sb(f"PT{u}", [P, 512]) for u in range(2)]
        rl = sb("rl", [P, 2, NHEAD])
        mix = sb("mix", [P, 2, C])
        mixT = sb("mixT", [P, CC, T])

        x_loaded, tok_loaded, w_loaded = sem("x_loaded"), sem("tok_loaded"), sem("w_loaded")
        const_set, const_ready = sem("const_set"), sem("const_ready")
        dve_own = sem("dve_own")
        var_ready, rstd_ready = sem("var_ready"), sem("rstd_ready")
        xn_ready, xT_psum, xT_ready, proj_ready, e_ready = (
            sem("xn_ready"), sem("xT_psum"), sem("xT_ready"), sem("proj_ready"), sem("e_ready"))
        sh_ready, mask_ready, weights_ready = sem("sh_ready"), sem("mask_ready"), sem("weights_ready")
        empty_set, table_set, ids_set = sem("empty_set"), sem("table_set"), sem("ids_set")
        chosen_ready, slot_psum, slot_ready, shT_psum, shT_ready = (
            sem("chosen_ready"), sem("slot_psum"), sem("slot_ready"), sem("shT_psum"), sem("shT_ready"))
        shd_psum, x_shared = sem("shd_psum"), sem("x_shared")
        row_ready, dispatched, meta_ready, idx_ready = sem("row_ready"), sem("dispatched"), sem("meta_ready"), sem("idx_ready")
        slots_loaded = [sem("slots_loaded0"), sem("slots_loaded1")]
        t0_psum, t1_psum, xd0_ready, xd1_ready = (
            sem("t0_psum"), sem("t1_psum"), sem("xd0_ready"), sem("xd1_ready"))
        up_psum, eg_ready, h_ready, hT_psum, hT_ready = (
            sem("up_psum"), sem("eg_ready"), sem("h_ready"), sem("hT_psum"), sem("hT_ready"))
        y_psum, ya_ready, yb_ready = sem("y_psum"), sem("ya_ready"), sem("yb_ready")
        acc_set = [sem("acc_set0"), sem("acc_set1")]
        acc_done = [sem("acc_done0"), sem("acc_done1")]
        fin_loaded = [sem(f"fin_loaded{c}") for c in range(4)]
        summed, stored = sem("summed"), sem("stored")
        aw_loaded, gate_exp, gate_ready = sem("aw_loaded"), sem("gate_exp"), sem("gate_ready")
        xn2_ready, xT2_psum, xT2_ready = sem("xn2_ready"), sem("xT2_psum"), sem("xT2_ready")
        q_psum, q_ready, k_psum, k_ready, v_psum, v_ready = (
            sem("q_psum"), sem("q_ready"), sem("k_psum"), sem("k_ready"), sem("v_psum"), sem("v_ready"))
        expq_ready, sigma_ready = sem("expq_ready"), sem("sigma_ready")
        pool_own = sem("pool_own")
        thirds_ready, thirds_stored = sem("thirds_ready"), sem("thirds_stored")
        stacked = [sem("stacked0"), sem("stacked1")]
        raw_psum, raw_ready, rel_psum, rel_ready, wm_ready = (
            sem("raw_psum"), sem("raw_ready"), sem("rel_psum"), sem("rel_ready"), sem("wm_ready"))
        mem_psum, mem_used = sem("mem_psum"), sem("mem_used")
        s_psum, max_ready, p_ready, pt_psum, pt_ready, pv_done = (
            sem("s_psum"), sem("max_ready"), sem("p_ready"), sem("pt_psum"), sem("pt_ready"), sem("pv_done"))
        mix_ready, mixT_psum, mixT_ready, wo_psum, wo_used = (
            sem("mix_ready"), sem("mixT_psum"), sem("mixT_ready"), sem("wo_psum"), sem("wo_used"))

        ZPARTS = NT // 4 + 1
        INIT = [16 * NT, 16 * ZPARTS]
        ADDS = 16 * E // 2

        block = ctx.enter_context(nc.Block())

        @block.sync
        def _(sp):
            x_t = x_in.rearrange("(t p) c -> p t c", p=P)
            out_t = out.rearrange("(t p) c -> p t c", p=P)
            slots_t = table[0:SLOTS, :].rearrange("(e p) c -> p e c", p=P)
            empty = zrow[:].rearrange("p (o c) -> p o c", o=1)
            acc_t = [a[0:N, :].rearrange("(t p) c -> p t c", p=P) for a in acc]
            sp.dma_start(X[:], x_t).then_inc(x_loaded, 16)
            sp.dma_start(wtok[:], w_tok).then_inc(tok_loaded, 16)
            sp.dma_start(wsd[:], w_shared_down).then_inc(tok_loaded, 16)
            sp.wait_ge(empty_set, 2)
            for c in range(8):
                sp.dma_start(slots_t[:, 8 * c:8 * c + 8, :], empty.to_broadcast([P, 8, ROW])).then_inc(table_set, 16)
            sp.dma_start(wup[:], w_up).then_inc(w_loaded, 16)
            sp.dma_start(wdn[:], w_down).then_inc(w_loaded, 16)
            for w, src in ((wq, w_q), (wk, w_k), (wv, w_v), (wo, w_o), (mems, memories), (nrm, norms)):
                sp.dma_start(w[:], src).then_inc(aw_loaded, 16)
            sp.dma_start(gt[:, 0:1], gate.to_broadcast([P, 1])).then_inc(aw_loaded, 16)

            def moe(f):
                if f:
                    sp.wait_ge(fin_loaded[3], 32)
                    for c in range(3):
                        sp.wait_ge(fin_loaded[c], 32)
                zeros = zrow[:, 0:C].rearrange("p (o c) -> p o c", o=1)
                for c in range(ZPARTS):
                    part_ = acc[1][4 * P * c:min(4 * P * (c + 1), DUMP), :].rearrange("(t p) c -> p t c", p=P)
                    sp.dma_start(part_, zeros.to_broadcast(list(part_.shape))).then_inc(acc_set[1], 16)
                if not f:
                    sp.dma_start(acc[0][N:DUMP, :], zrow[:, 0:C]).then_inc(w_loaded, 16)

                with sp.Fori(0, NT) as t:
                    sp.wait_ge(x_shared, t + NT * f + 1)
                    sp.dma_start(acc_t[0][:, bass.ds(t, 1), :], X[:, bass.ds(t, 1), :]).then_inc(acc_set[0], 16)

                def load_group(i, u):
                    sp.dma_start(xg[u][:], slots_t[:, bass.ds(EG * (2 * i + u), EG), :]).then_inc(slots_loaded[u], 16)

                sp.wait_ge(dispatched, 16 * TOPK * NT * (f + 1))
                load_group(0, 0)
                load_group(0, 1)
                with sp.Fori(1, NG // 2) as i:
                    for u in range(2):
                        sp.wait_ge(t1_psum, 2 * i + (u - 1 + NG * f))
                        sp.wait_ge(meta_ready, 2 * i + (u - 1 + NG * f))
                        load_group(i, u)
                for r in range(2):
                    sp.wait_ge(acc_done[r], ADDS * (f + 1))
                for c in range(4):
                    tiles = slice(4 * c, 4 * c + 4)
                    sp.dma_start(X[:, tiles, :], acc_t[0][:, tiles, :]).then_inc(fin_loaded[c], 16)
                    sp.dma_start(fin[:, tiles, :], acc_t[1][:, tiles, :]).then_inc(fin_loaded[c], 16)

            def stack(b, u):
                for w, (name, slots) in enumerate(((QS, Q_SLOTS), (KS, K_SLOTS))):
                    sp.wait_ge(thirds_ready, 2 * b + w + 1)
                    if u_first(b):
                        pass
                    else:
                        sp.wait_ge(stacked[u], (b - u) * (8 * 2 * len(Q_SLOTS)))
                    for k in range(3):
                        sp.dma_start(thirds[u, w, k].rearrange("(c p) t -> p c t", p=P),
                                     part[w][:, k, :].rearrange("p (c t) -> p c t", c=CC)).then_inc(thirds_stored, 16)
                    sp.wait_ge(thirds_stored, (2 * b + w + 1) * 48)
                    if not u_first(b):
                        sp.wait_ge(s_psum, (b - 1) * UNITS)
                    for s_, k in enumerate(slots):
                        sp.dma_start(name[u][HD * s_:HD * s_ + HD, :, :],
                                     thirds[u, w, k].rearrange("(h d) t -> d h t", d=HD)).then_inc(stacked[u], 16)

            def u_first(b):
                return isinstance(b, int) and b < 2

            def attention_():
                for b in range(B):
                    stack(b, b % 2)
                    if b == 1:
                        for c in range(8):
                            sp.dma_start(slots_t[:, 8 * c:8 * c + 8, C:],
                                         empty[:, :, C:].to_broadcast([P, 8, META])).then_inc(table_set, 16)

            for f in range(layers):
                moe(f)
                if attention and f == 0:
                    attention_()
            for c in range(4):
                sp.wait_ge(summed, NT * (layers - 1) + 4 * c + 4)
                tiles = slice(4 * c, 4 * c + 4)
                sp.dma_start(out_t[:, tiles, :], X[:, tiles, :]).then_inc(stored, 16)
            sp.wait_ge(stored, 64)

        @block.gpsimd
        def _(pool):
            g = nc.gpsimd
            g.memset(zrow[:, 0:ROW - 1], 0.0).then_inc(empty_set, 1)
            g.iota(zrow[:, ROW - 1:ROW], [[0, 1]], base=N, channel_multiplier=1,
                   allow_small_or_imprecise_dtypes=True).then_inc(empty_set, 1)
            g.memset(causal[:], 0.0).then_inc(pool_own, 1)
            g.memset(mean_w[:], 1.0 / T).then_inc(const_ready, 1)
            for u in range(2):
                g.memset(V[u][:], 1.0).then_inc(const_ready, 1)
            for m in (ident, identb, hbig[0], hbig[1]):
                g.memset(m[:], 0.0).then_inc(const_set, 1)
            g.memset(minus_half[:], -0.5).then_inc(const_set, 1)
            g.memset(before[:], 1.0).then_inc(const_set, 1)
            g.memset(ones[:], 1.0).then_inc(const_set, 1)
            for m, step, base in ((expert_no, 1, 0), (slot_end, CAP, CAP)):
                g.iota(m[:], [[step, E]], base=base, channel_multiplier=0,
                       allow_small_or_imprecise_dtypes=True).then_inc(const_set, 1)
            g.iota(over_row[:], [[P, NT * TOPK]], base=SLOTS + 1, channel_multiplier=1,
                   allow_small_or_imprecise_dtypes=True).then_inc(const_set, 1)
            pool.wait_ge(const_set, 10)
            g.affine_select(out=before[:], in_=before[:], compare_op=ALU.is_gt, fill=0.0, base=0,
                            pattern=[[1, P]], channel_multiplier=-1).then_inc(const_ready, 1)
            for m in (ident, identb):
                g.affine_select(out=m[:], in_=m[:], compare_op=ALU.not_equal, fill=1.0, base=0,
                                pattern=[[-1, P]], channel_multiplier=1).then_inc(const_ready, 1)
            pool.wait_ge(pool_own, 1)
            g.affine_select(out=causal[:], in_=causal[:], compare_op=ALU.is_ge, fill=-1e9, base=0,
                            pattern=[[0, 4], [-1, P]], channel_multiplier=1).then_inc(const_ready, 1)

            def moe(f):
                pool.wait_ge(var_ready, 2 * f + 1)
                g.tensor_tensor(rstd[:], ve[:], minus_half[:], ALU.pow).then_inc(rstd_ready, 1)
                g.iota(rows[:, :, ROW - 1], [[P, NT]], base=0, channel_multiplier=1,
                       allow_small_or_imprecise_dtypes=True).then_inc(ids_set, 1)
                pool.wait_ge(ids_set, f + 1)
                pool.wait_ge(table_set, 128 * (f + 1))

                for t in range(NT):
                    pool.wait_ge(row_ready, t + 1 + NT * f)
                    pool.wait_ge(weights_ready, t + 1 + NT * f)
                    pool.wait_ge(slot_ready, t + 1 + NT * f)
                    for k in range(TOPK):
                        g.indirect_dma_start(out=table[:, :],
                                             out_offset=bass.IndirectOffsetOnAxis(slot[:, t, k:k + 1], 0),
                                             in_=rows[:, t, :], in_offset=None).then_inc(dispatched, 16)

                for r in range(2):
                    pool.wait_ge(acc_set[r], INIT[r] * (f + 1))
                for gi in range(NG):
                    for e in range(EG):
                        r = e % 2
                        if e == 0:
                            pool.wait_ge(idx_ready, gi + NG * f + 1)
                            pool.wait_ge(ya_ready, gi + NG * f + 1)
                        if e == 2:
                            pool.wait_ge(yb_ready, gi + NG * f + 1)
                        if 2 * gi + e // 2 > 0:
                            pool.wait_ge(acc_done[r], (2 * gi + e // 2) * 16 + ADDS * f)
                        g.indirect_dma_start(out=acc[r][:, :],
                                             out_offset=bass.IndirectOffsetOnAxis(IDX[:, EG * gi + e:EG * gi + e + 1], 0),
                                             in_=ysb[gi % 2][:, e, :], in_offset=None, compute_op=ALU.add)\
                         .then_inc(acc_done[r], 16)

            def thirds_of(src, ready, w, b):
                pool.wait_ge(ready, b + 1)
                if not (isinstance(b, int) and b == 0):
                    pool.wait_ge(thirds_stored, b * 96 - 48 + 48 * w)
                base = 1 + 8 * b + 4 * w
                g.tensor_copy(part[w][:, 0, :], src[:]).then_inc(pool_own, 1)
                pool.wait_ge(pool_own, base + 1)
                g.tensor_tensor(rest[w][:], src[:], part[w][:, 0, :], ALU.subtract).then_inc(pool_own, 1)
                pool.wait_ge(pool_own, base + 2)
                g.tensor_copy(part[w][:, 1, :], rest[w][:]).then_inc(pool_own, 1)
                pool.wait_ge(pool_own, base + 3)
                g.tensor_tensor(rest[w][:], rest[w][:], part[w][:, 1, :], ALU.subtract).then_inc(pool_own, 1)
                pool.wait_ge(pool_own, base + 4)
                g.tensor_copy(part[w][:, 2, :], rest[w][:]).then_inc(thirds_ready, 1)

            def attention_():
                pool.wait_ge(var_ready, 2)
                g.tensor_tensor(rstd[:], ve[:], minus_half[:], ALU.pow).then_inc(rstd_ready, 1)
                for b in range(B):
                    thirds_of(qT, q_ready, 0, b)
                    thirds_of(kT, k_ready, 1, b)

            for f in range(layers):
                moe(f)
                if attention and f == 0:
                    attention_()

        @block.scalar
        def _(act):
            a = nc.scalar

            def moe(f):
                def copy_xT(i, u):
                    s = 2 * i + u + NT * f
                    act.wait_ge(xn_ready, s + 1)
                    a.activation(rows[:, bass.ds(2 * i + u, 1), 0:C].rearrange("p o c -> p (o c)"), xn[:, u, :], ACT.Copy)\
                     .then_inc(row_ready, 1)
                    act.wait_ge(xT_psum, s + 1)
                    a.activation(xT[:, u, :], bank[u][:, 0:CC * P], ACT.Copy).then_inc(xT_ready, 1)

                def exp_gates(i, u):
                    s = 2 * i + u + NT * f
                    act.wait_ge(proj_ready, s + 1)
                    a.activation(en[:, u, :], bank[2 + u][:, HS:2 * HS + E], ACT.Exp, scale=-1.0).then_inc(e_ready, 1)

                def copy_shT(i, u):
                    s = 2 * i + u + NT * f
                    act.wait_ge(shT_psum, s + 1)
                    a.activation(shT[:, u, :], bank[5][0:HS, 0:P], ACT.Copy).then_inc(shT_ready, 1)

                def step(i, u, last=False):
                    if not last:
                        copy_xT(i + u, 1 - u)
                        exp_gates(i + u, 1 - u)
                    copy_shT(i, u)

                copy_xT(0, 0)
                exp_gates(0, 0)
                with act.Fori(0, HALF - 1) as i:
                    step(i, 0)
                    step(i, 1)
                step(HALF - 1, 0)
                step(HALF - 1, 1, last=True)

                def copy_xd(i, u):
                    act.wait_ge(slots_loaded[u], i * 16 + 16 * (NG // 2 * f + 1))
                    if not (isinstance(i, int) and 2 * i + u < 2 and not f):
                        act.wait_ge(h_ready, 2 * i + u + NG * f - 1)
                    a.activation(meta[u][:], xg[u][:, :, C:ROW], ACT.Copy).then_inc(meta_ready, 1)
                    act.wait_ge(t0_psum, 2 * i + u + NG * f + 1)
                    a.activation(xdT[u][:, 0, :], bank[0][:], ACT.Copy).then_inc(xd0_ready, 1)

                def copy_hT(i, u):
                    act.wait_ge(hT_psum, 2 * i + u + NG * f + 1)
                    a.activation(hT[u][:], bank[4][:], ACT.Copy).then_inc(hT_ready, 1)

                def exp_up(i, u):
                    act.wait_ge(up_psum, 2 * i + u + NG * f + 1)
                    v = bank[2 + u][:, 0:EG * 2 * H].rearrange("p (e h) -> p e h", e=EG)
                    a.activation(eg[u][:], v[:, :, 0:H], ACT.Exp, scale=-1.0).then_inc(eg_ready, 1)

                def copy_y(i, u):
                    act.wait_ge(y_psum, 2 * i + u + NG * f + 1)
                    if not (isinstance(i, int) and i == 0):
                        act.wait_ge(acc_done[0], i * 64 + (32 * u - 48 + ADDS * f))
                        act.wait_ge(acc_done[1], i * 64 + (32 * u - 48 + ADDS * f))
                    a.activation(ysb[u][:, 0:2, :], bank[5][:].rearrange("p (e c) -> p e c", e=2), ACT.Copy)\
                     .then_inc(ya_ready, 1)

                def estep(i, u, last=False):
                    if not last:
                        copy_xd(i + u, 1 - u)
                    copy_hT(i, u)
                    if not last:
                        exp_up(i + u, 1 - u)
                    copy_y(i, u)

                copy_xd(0, 0)
                exp_up(0, 0)
                estep(0, 0)
                estep(0, 1)
                with act.Fori(1, NG // 2 - 1) as i:
                    estep(i, 0)
                    estep(i, 1)
                estep(NG // 2 - 1, 0)
                estep(NG // 2 - 1, 1, last=True)

            def exps(b, u, n):
                U = UNITS * b + n
                need(act, max_ready, U + 1)
                need(act, pt_psum, U - 1)
                k = 4 if n % 3 == 0 else 2
                w = 512 // k
                for i in range(k):
                    last = a.activation(Pr[n % 2][:, w * i:w * i + w], bank[n % 2][:, w * i:w * i + w], ACT.Exp,
                                        bias=negmax[n % 2][:, i:i + 1])
                last.then_inc(p_ready, 1)

            def copy_qT(b, u):
                act.wait_ge(q_psum, b + 1)
                need(act, thirds_ready, 2 * b - 1)
                need(act, sigma_ready, b)
                a.activation(qT[:], bank[6][:], ACT.Copy).then_inc(q_ready, 1)
                act.wait_ge(q_ready, b + 1)
                a.activation(sigma[u][:].rearrange("p c t -> p (c t)"), qT[:], ACT.Exp).then_inc(expq_ready, 1)

            def copy_kT(b):
                act.wait_ge(k_psum, b + 1)
                need(act, thirds_ready, 2 * b)
                a.activation(kT[:], bank[6][:], ACT.Copy, scale=HD ** -0.5).then_inc(k_ready, 1)

            def copy_xT2(b):
                act.wait_ge(xT2_psum, b + 1)
                a.activation(xT2[:].rearrange("p c t -> p (c t)"), bank[7][:], ACT.Copy).then_inc(xT2_ready, 1)

            def copy_v(b, u):
                act.wait_ge(v_psum, b + 1)
                a.activation(V[u][:, :, :, 0:HD], bank[6][:].rearrange("p (t h d) -> p t h d", t=2, h=NHEAD), ACT.Copy)\
                 .then_inc(v_ready, 1)

            def body(b, u, first=False, last=False):
                for n in range(UNITS):
                    if n == 1 and not last:
                        copy_xT2(b + 1)
                    if n == 2:
                        act.wait_ge(rel_ready, b + 1)
                        a.activation(wm[:, 0:MEM], rel[:], ACT.Exp, bias=wsc[:, 0:1], accum_out=wsc[:, 1:2])\
                         .then_inc(wm_ready, 1)
                        if not last:
                            copy_qT(b + 1, 1 - u)
                    if n == 3 and not first:
                        act.wait_ge(mixT_psum, b)
                        a.activation(mixT[:].rearrange("p c t -> p (c t)"), bank[7][:], ACT.Copy).then_inc(mixT_ready, 1)
                    if n == 4 and not last:
                        copy_kT(b + 1)
                    if n == 6 and not last:
                        copy_v(b + 1, 1 - u)
                    exps(b, u, n)

            def attention_():
                act.wait_ge(aw_loaded, 112)
                a.activation(gt[:, 1:2], gt[:, 0:1], ACT.Exp, scale=-1.0).then_inc(gate_exp, 1)
                copy_xT2(0)
                copy_qT(0, 0)
                copy_kT(0)
                copy_v(0, 0)
                body(0, 0, first=True)
                with act.Fori(0, B // 2 - 1) as i:
                    body(2 * i + 1, 1)
                    body(2 * i + 2, 0)
                body(B - 1, 1, last=True)
                act.wait_ge(mixT_psum, B)
                a.activation(mixT[:].rearrange("p c t -> p (c t)"), bank[7][:], ACT.Copy).then_inc(mixT_ready, 1)

            for f in range(layers):
                moe(f)
                if attention and f == 0:
                    attention_()

        @block.vector
        def _(dve):
            v = nc.vector
            own = Own(dve, dve_own)

            def stats(t):
                own.mark(v.bn_stats(st[:, t, :], X[:, t, :]))

            def variance():
                own.settle()
                own.mark(v.tensor_tensor(mean[:], st[:, :, 1], st[:, :, 4], ALU.add))
                own.mark(v.tensor_tensor(dev[:], st[:, :, 1], st[:, :, 4], ALU.subtract))
                own.link(v.tensor_tensor(ve[:], st[:, :, 2], st[:, :, 5], ALU.add))
                own.mark(v.tensor_scalar(mean[:], mean[:], 0.5, None, ALU.mult))
                own.mark(v.tensor_scalar(ve[:], ve[:], 1.0 / C, LN_EPS, ALU.mult, ALU.add))
                own.link(v.scalar_tensor_tensor(dev[:], dev[:], 0.25, dev[:], ALU.mult, ALU.mult))
                v.tensor_tensor(ve[:], ve[:], dev[:], ALU.add).then_inc(var_ready, 1)

            own.mark(v.memset(sg[:, 0, HS + E:], -1.0))
            own.mark(v.memset(sg[:, 1, HS + E:], -1.0))
            dve.wait_ge(const_set, 10)
            dve.wait_ge(x_loaded, 16)
            with own.loop(0, NT, 1) as t:
                stats(t)
            variance()

            def moe(f):
                dve.wait_ge(rstd_ready, 2 * f + 1 if attention else f + 1)

                v.tensor_copy(chosen[:], expert_no[:]).then_inc(chosen_ready, 1)

                def normalise(i, u):
                    t = 2 * i + u
                    if f or not (isinstance(i, int) and i == 0):
                        dve.wait_ge(xT_psum, t + NT * f - 1)
                        dve.wait_ge(row_ready, t + NT * f - 1)
                    v.tensor_scalar(xn[:, u, :], X[:, bass.ds(t, 1), :].rearrange("p o c -> p (o c)"), mean[:, bass.ds(t, 1)],
                                    rstd[:, bass.ds(t, 1)], ALU.subtract, ALU.mult).then_inc(xn_ready, 1)

                def route(i, u):
                    s = 2 * i + u + NT * f
                    proj = bank[2 + u]
                    dve.wait_ge(e_ready, s + 1)
                    own.link(v.tensor_scalar_add(sg[:, u, 0:HS + E], en[:, u, :], 1.0))
                    own.link(v.reciprocal(sg[:, u, 0:HS + E], sg[:, u, 0:HS + E]))
                    own.mark(v.tensor_tensor(sh1[:], proj[:, HS:2 * HS], sg[:, u, 0:HS], ALU.mult))
                    own.link(v.max(top8[:], sg[:, u, HS:HS + E]))
                    v.tensor_tensor(sh[:, u, :], proj[:, 0:HS], sh1[:], ALU.mult).then_inc(sh_ready, 1)
                    own.mark(v.reduce_sum(ssum[:, 0:1], top8[:, 0:TOPK], AX.X))
                    own.link(v.memset(top8[:, TOPK:8], -1.0))
                    own.mark(v.reciprocal(ssum[:, 1:2], ssum[:, 0:1]))
                    own.link(v.match_replace(rep[:], top8[:], sg[:, u, HS:], -1.0))
                    v.tensor_tensor(mask[:, u, :], rep[:, 0:E], sg[:, u, HS:HS + E], ALU.is_lt).then_inc(mask_ready, 1)
                    own.link(v.tensor_scalar(ssum[:, 2:3], ssum[:, 1:2], 0.5, None, ALU.mult))
                    dve.wait_ge(mask_ready, s + 1)
                    own.mark(v.tensor_tensor(end_of[:, u, :], slot_end[:], mask[:, u, :], ALU.mult))
                    v.scalar_tensor_tensor(rows[:, bass.ds(2 * i + u, 1), C:C + E].rearrange("p o c -> p (o c)"),
                                           sg[:, u, HS:HS + E], ssum[:, 2:3], mask[:, u, :],
                                           ALU.mult, ALU.mult).then_inc(weights_ready, 1)

                def place(i, u):
                    t = 2 * i + u
                    s = t + NT * f
                    at = bank[4][:, 0:E]
                    dve.wait_ge(slot_psum, s + 1)
                    own.link(v.tensor_tensor(fits[:], at, end_of[:, u, :], ALU.is_lt))
                    own.link(v.scalar_tensor_tensor(key[:], at, 1.0, fits[:], ALU.add, ALU.mult))
                    v.tensor_tensor(chosen[:], chosen[:], mask[:, u, :], ALU.add).then_inc(chosen_ready, 1)
                    own.link(v.max(key8[:], key[:]))
                    own.link(v.scalar_tensor_tensor(over[:], key8[:, 0:TOPK], 0.0, over_row[:, bass.ds(TOPK * t, TOPK)],
                                                    ALU.is_equal, ALU.mult))
                    v.scalar_tensor_tensor(slot[:, bass.ds(t, 1), :].rearrange("p o k -> p (o k)"), key8[:, 0:TOPK], -1.0,
                                           over[:], ALU.add, ALU.add).then_inc(slot_ready, 1)

                def add_shared(i, u):
                    t = 2 * i + u
                    x = X[:, bass.ds(t, 1), :].rearrange("p o c -> p (o c)")
                    dve.wait_ge(shd_psum, t + NT * f + 1)
                    v.scalar_tensor_tensor(x, bank[6 + u][:, 0:C], 0.5, x, ALU.mult, ALU.add)\
                     .then_inc(x_shared, 1)

                normalise(0, 0)
                normalise(0, 1)
                route(0, 0)
                with own.loop(0, HALF - 1, 28) as i:
                    normalise(i + 1, 0)
                    route(i, 1)
                    place(i, 0)
                    add_shared(i, 0)
                    normalise(i + 1, 1)
                    route(i + 1, 0)
                    place(i, 1)
                    add_shared(i, 1)
                route(HALF - 1, 1)
                place(HALF - 1, 0)
                add_shared(HALF - 1, 0)
                place(HALF - 1, 1)
                add_shared(HALF - 1, 1)

                def copy_xd(i, u):
                    dve.wait_ge(t1_psum, 2 * i + u + NG * f + 1)
                    v.tensor_copy(xdT[u][:, 1, :], bank[1][:]).then_inc(xd1_ready, 1)

                def hidden(i, u):
                    gi = 2 * i + u
                    dve.wait_ge(meta_ready, gi + NG * f + 1)
                    v.tensor_copy(IDX[:, bass.ds(EG * gi, EG)], meta[u][:, :, META - 1]).then_inc(idx_ready, 1)
                    up = bank[2 + u][:, 0:EG * 2 * H].rearrange("p (e h) -> p e h", e=EG)
                    dve.wait_ge(eg_ready, gi + NG * f + 1)
                    own.link(v.tensor_scalar_add(eg[u][:], eg[u][:], 1.0))
                    own.link(v.reciprocal(eg[u][:], eg[u][:]))
                    own.link(v.tensor_tensor(eg[u][:], up[:, :, 0:H], eg[u][:], ALU.mult))
                    own.link(v.tensor_tensor(eg[u][:], up[:, :, H:], eg[u][:], ALU.mult))
                    for e in range(EG):
                        last = v.tensor_scalar(hbig[u][:, e * P + e * H:e * P + e * H + H], eg[u][:, e, :],
                                               meta[u][:, e, bass.ds(EG * gi + e, 1)], None, ALU.mult)
                        if e < EG - 1:
                            own.mark(last)
                    last.then_inc(h_ready, 1)

                def copy_y(i, u):
                    dve.wait_ge(y_psum, 2 * i + u + NG * f + 1)
                    if not (isinstance(i, int) and i == 0):
                        dve.wait_ge(acc_done[0], i * 64 + (32 * u - 32 + ADDS * f))
                        dve.wait_ge(acc_done[1], i * 64 + (32 * u - 32 + ADDS * f))
                    v.tensor_copy(ysb[u][:, 2:4, :], bank[6][:].rearrange("p (e c) -> p e c", e=2)).then_inc(yb_ready, 1)

                def estep(i, u, last=False):
                    if not last:
                        copy_xd(i + u, 1 - u)
                        hidden(i + u, 1 - u)
                    copy_y(i, u)

                copy_xd(0, 0)
                hidden(0, 0)
                estep(0, 0)
                estep(0, 1)
                with own.loop(1, NG // 2 - 1, 14) as i:
                    estep(i, 0)
                    estep(i, 1)
                estep(NG // 2 - 1, 0)
                estep(NG // 2 - 1, 1, last=True)

                for c in range(4):
                    dve.wait_ge(fin_loaded[c], 32 * (f + 1))
                    with own.loop(4 * c, 4 * c + 4, 1 if f + 1 < layers else 0) as t:
                        v.tensor_tensor(X[:, t, :], X[:, t, :], fin[:, t, :], ALU.add).then_inc(summed, 1)
                        if f + 1 < layers:
                            dve.wait_ge(summed, NT * f + t + 1)
                            stats(t)
                if f + 1 < layers:
                    variance()

            def rowmax(b, n):
                U = UNITS * b + n
                k = 4 if n % 3 == 0 else 2
                dve.wait_ge(s_psum, U + 1)
                v.tensor_reduce(negmax[n % 2][:, 0:k], bank[n % 2][:].rearrange("p (h t) -> p h t", h=k), AX.X, ALU.max,
                                negate=True).then_inc(max_ready, 1)

            def copy_pt(U, n):
                dve.wait_ge(pt_psum, U + 1)
                need(dve, pv_done, U - 1)
                v.tensor_copy(PT[n % 2][:], bank[2 + n % 2][:]).then_inc(pt_ready, 1)

            def normalise2(b):
                for t in range(2):
                    last = v.tensor_scalar(xn[:, t, :], X[:, 2 * b + t, :], mean[:, bass.ds(2 * b + t, 1)],
                                           rstd[:, bass.ds(2 * b + t, 1)], ALU.subtract, ALU.mult)
                    last.then_inc(xn2_ready, 1)

            def sigmas(b, u):
                flat = sigma[u][:].rearrange("p c t -> p (c t)")
                dve.wait_ge(expq_ready, b + 1)
                own.link(v.tensor_scalar(flat, flat, 1.0, None, ALU.min))
                v.scalar_tensor_tensor(flat, qT[:], 0.0, flat, ALU.max, ALU.add).then_inc(sigma_ready, 1)

            def raws(b):
                dve.wait_ge(raw_psum, b + 1)
                v.tensor_copy(raw[:].rearrange("p t m -> p (t m)"), bank[6][:, 0:2 * MEM]).then_inc(raw_ready, 1)

            def rels(b):
                dve.wait_ge(rel_psum, b + 1)
                own.link(v.tensor_copy(rel[:], bank[6][:, 16:16 + MEM]))
                v.tensor_reduce(wsc[:, 0:1], rel[:], AX.X, ALU.max, negate=True).then_inc(rel_ready, 1)

            def coefs(b):
                own.link(v.tensor_scalar(rawc[:], raw[:], CLIP, None, ALU.max))
                own.link(v.reciprocal(rawc[:], rawc[:]))
                dve.wait_ge(wm_ready, b + 1)
                own.link(v.reciprocal(wsc[:, 2:3], wsc[:, 1:2]))
                own.link(v.tensor_scalar(wm[:, MEM:], wm[:, 0:MEM], wsc[:, 2:3], gt[:, 2:3], ALU.mult, ALU.mult))
                for t in range(2):
                    own.mark(v.tensor_tensor(coef[:, t, :], rawc[:, t, :], wm[:, MEM:], ALU.mult))

            def mem_sum(b, j):
                t, half = j // 2, j % 2
                if j == 0:
                    own.settle()
                dve.wait_ge(mem_psum, 4 * b + j + 1)
                pm = bank[6 + (7 + j) % 2]
                for k in range(2):
                    src, c = pm[:, C * k:C * k + C], coef[:, t, 2 * half + k:2 * half + k + 1]
                    if half == 0 and k == 0:
                        own.link(v.tensor_scalar(memo[:, t, :], src, c, None, ALU.mult))
                    elif k == 0:
                        own.link(v.scalar_tensor_tensor(memo[:, t, :], src, c, memo[:, t, :], ALU.mult, ALU.add))
                    else:
                        v.scalar_tensor_tensor(memo[:, t, :], src, c, memo[:, t, :], ALU.mult, ALU.add)\
                         .then_inc(mem_used, 1)
                        if half == 0:
                            dve.wait_ge(mem_used, 4 * b + j + 1)

            def finalise(b):
                dve.wait_ge(pv_done, UNITS * b + UNITS)
                o = [bank[4 + t][:, 0:NHEAD * (HD + 1)].rearrange("p (h d) -> p h d", h=NHEAD) for t in range(2)]
                for t in range(2):
                    own.mark(v.reciprocal(rl[:, t, :], o[t][:, :, HD]))
                own.settle()
                own.link(v.tensor_scalar(rl[:], rl[:], gt[:, 3:4], None, ALU.mult))
                for t in range(2):
                    w = rl[:, t, :].rearrange("p (h o) -> p h o", o=1).to_broadcast([P, NHEAD, HD])
                    own.mark(v.tensor_tensor(mix[:, t, :].rearrange("p (h d) -> p h d", h=NHEAD), o[t][:, :, 0:HD], w,
                                             ALU.mult))
                own.settle()
                dve.wait_ge(mem_used, 4 * b + 4)
                v.tensor_tensor(mix[:], mix[:], memo[:], ALU.add).then_inc(mix_ready, 1)

            def residual(b):
                dve.wait_ge(wo_psum, b + 1)
                x2 = X[:, bass.ds(2 * b, 2), :]
                v.tensor_tensor(x2, x2, bank[7][:].rearrange("p (t c) -> p t c", t=2), ALU.add).then_inc(wo_used, 1)
                dve.wait_ge(wo_used, b + 1)
                stats(2 * b)
                stats(2 * b + 1)

            def body(b, u, first=False, last=False):
                for n in range(UNITS):
                    U = UNITS * b + n
                    rowmax(b, n)
                    if n or not first:
                        copy_pt(U - 1, (n - 1) % UNITS)
                    if n == 0:
                        raws(b)
                        if not last:
                            normalise2(b + 1)
                    if n == 1:
                        rels(b)
                    if n == 2 and not first:
                        finalise(b - 1)
                    if n == 3 and not last:
                        sigmas(b + 1, 1 - u)
                    if n == 4:
                        coefs(b)
                    if n == 5 and not first:
                        residual(b - 1)
                    if 7 <= n < 11:
                        mem_sum(b, n - 7)

            def attention_():
                dve.wait_ge(gate_exp, 1)
                own.link(v.tensor_scalar_add(gt[:, 1:2], gt[:, 1:2], 1.0))
                own.link(v.reciprocal(gt[:, 2:3], gt[:, 1:2]))
                own.link(v.tensor_scalar(gt[:, 3:4], gt[:, 2:3], -1.0, 1.0, ALU.mult, ALU.add))
                dve.wait_ge(rstd_ready, 2)
                normalise2(0)
                sigmas(0, 0)
                body(0, 0, first=True)
                with own.loop(0, B // 2 - 1, 2 * 19) as i:
                    body(2 * i + 1, 1)
                    body(2 * i + 2, 0)
                body(B - 1, 1, last=True)
                copy_pt(UNITS * B - 1, UNITS - 1)
                finalise(B - 1)
                residual(B - 1)
                variance()

            for f in range(layers):
                moe(f)
                if attention and f == 0:
                    attention_()

        @block.tensor
        def _(pe):
            m = nc.tensor
            pe.wait_ge(const_ready, 7)
            pe.wait_ge(tok_loaded, 32)

            def moe(f):
                def project(i, u):
                    s = 2 * i + u + NT * f
                    pe.wait_ge(xn_ready, s + 1)
                    for c in range(CC):
                        last = m.transpose(bank[u][:, P * c:P * c + P], xn[:, u, P * c:P * c + P], ident[:])
                    last.then_inc(xT_psum, 1)
                    pe.wait_ge(xT_ready, s + 1)
                    for c in range(CC):
                        last = m.matmul(bank[2 + u][:, 0:2 * HS + E], xT[:, u, P * c:P * c + P], wtok[:, c, :],
                                        start=(c == 0), stop=(c == CC - 1))
                    last.then_inc(proj_ready, 1)

                def turn(i, u):
                    t = 2 * i + u
                    s = t + NT * f
                    pe.wait_ge(sh_ready, s + 1)
                    pe.wait_ge(mask_ready, s + 1)
                    pe.wait_ge(chosen_ready, t + ((NT + 1) * f + 1))
                    m.matmul(bank[4][:, 0:E], ones[:], chosen[:], start=True, stop=False)
                    m.matmul(bank[4][:, 0:E], before[:], mask[:, u, :], start=False, stop=True)\
                     .then_inc(slot_psum, 1)
                    m.transpose(bank[5][0:HS, 0:P], sh[:, u, :], ident[:]).then_inc(shT_psum, 1)

                def shared_down(i, u):
                    s = 2 * i + u + NT * f
                    pe.wait_ge(shT_ready, s + 1)
                    m.matmul(bank[6 + u][:, 0:C], shT[:, u, :], wsd[:], start=True, stop=True).then_inc(shd_psum, 1)

                project(0, 0)
                project(0, 1)
                turn(0, 0)
                shared_down(0, 0)
                with pe.Fori(0, HALF - 1) as i:
                    project(i + 1, 0)
                    turn(i, 1)
                    shared_down(i, 1)
                    project(i + 1, 1)
                    turn(i + 1, 0)
                    shared_down(i + 1, 0)
                turn(HALF - 1, 1)
                shared_down(HALF - 1, 1)

                def turn_rows(i, u):
                    gi = 2 * i + u
                    pe.wait_ge(slots_loaded[u], i * 16 + 16 * (NG // 2 * f + 1))
                    for c, sem_ in enumerate((t0_psum, t1_psum)):
                        for e in range(EG):
                            last = m.transpose(bank[c][:, P * e:P * e + P], xg[u][:, e, P * c:P * c + P], ident[:])
                        last.then_inc(sem_, 1)

                def up(i, u):
                    gi = 2 * i + u
                    pe.wait_ge(xd0_ready, gi + NG * f + 1)
                    pe.wait_ge(xd1_ready, gi + NG * f + 1)
                    for e in range(EG):
                        for c in range(CC):
                            last = m.matmul(bank[2 + u][:, 2 * H * e:2 * H * e + 2 * H], xdT[u][:, c, P * e:P * e + P],
                                            wup[:, c, EG * gi + e, :], start=(c == 0), stop=(c == CC - 1))
                    last.then_inc(up_psum, 1)

                def turn_hidden(i, u):
                    pe.wait_ge(h_ready, 2 * i + u + NG * f + 1)
                    for e in range(EG):
                        last = m.transpose(bank[4][:, P * e:P * e + P], hbig[u][:, P * e:P * e + P], ident[:])
                    last.then_inc(hT_psum, 1)

                def down(i, u):
                    gi = 2 * i + u
                    pe.wait_ge(hT_ready, gi + NG * f + 1)
                    if f or not isinstance(i, int) or i > 0 or u > 0:
                        pe.wait_ge(ya_ready, gi + NG * f)
                        pe.wait_ge(yb_ready, gi + NG * f)
                    for e in range(EG):
                        last = m.matmul(bank[5 + e // 2][:, C * (e % 2):C * (e % 2) + C], hT[u][:, P * e:P * e + P],
                                        wdn[:, gi, :], start=True, stop=True)
                    last.then_inc(y_psum, 1)

                def estep(i, u, last=False):
                    if not last:
                        turn_rows(i + u, 1 - u)
                    turn_hidden(i, u)
                    if not last:
                        up(i + u, 1 - u)
                    down(i, u)

                pe.wait_ge(w_loaded, 48)
                turn_rows(0, 0)
                up(0, 0)
                estep(0, 0)
                with pe.Fori(0, NG // 2 - 1) as i:
                    estep(i, 1)
                    estep(i + 1, 0)
                estep(NG // 2 - 1, 1, last=True)

            def scores(b, u, n):
                U = UNITS * b + n
                if n == 0:
                    pe.wait_ge(stacked[u], (b - u + 2) * (8 * 2 * len(Q_SLOTS)))
                need(pe, p_ready, U - 1)
                hg, j = n // 3, n % 3
                out_, heads = bank[n % 2], range(4 * hg, 4 * hg + 4) if j == 0 else range(4 * hg + 2 * j - 2, 4 * hg + 2 * j)
                q0, w = (0, P) if j == 0 else (P, T)
                for i, h in enumerate(heads):
                    m.matmul(out_[:, w * i:w * i + w], QS[u][:, h, q0:q0 + P], KS[u][:, h, 0:w],
                             start=(i == 0), stop=False, skip_group_check=True)
                diag = out_[:].rearrange("p (h t) -> p h t", t=w)[:, :, w - P:w]
                m.matmul(diag, identb[:], causal[:, 0:len(heads), :], start=False, stop=True,
                         skip_group_check=True).then_inc(s_psum, 1)

            def turn_p(U, n):
                pe.wait_ge(p_ready, U + 1)
                need(pe, pt_ready, U - 1)
                for i in range(4):
                    last = m.transpose(bank[2 + n % 2][:, P * i:P * i + P], Pr[n % 2][:, P * i:P * i + P], ident[:])
                last.then_inc(pt_psum, 1)

            def values(b, u, n):
                U = UNITS * b + n
                pe.wait_ge(pt_ready, U + 1)
                if n == 0:
                    pe.wait_ge(v_ready, b + 1)
                    need(pe, mix_ready, b)
                hg, j = n // 3, n % 3
                for i in range(4):
                    h, t, kb = (4 * hg + i, 0, 0) if j == 0 else (4 * hg + 2 * j - 2 + i // 2, 1, i % 2)
                    last = m.matmul(bank[4 + t][:, (HD + 1) * h:(HD + 1) * h + HD + 1], PT[n % 2][:, P * i:P * i + P],
                                    V[u][:, kb, h, :], start=(kb == 0), stop=(kb == t))
                last.then_inc(pv_done, 1)

            def turn_x(b):
                pe.wait_ge(xn2_ready, 2 * b + 2)
                need(pe, mem_used, 4 * b - 4)
                for c in range(CC):
                    for t in range(2):
                        last = m.transpose(bank[7][:, T * c + P * t:T * c + P * t + P], xn[:, t, P * c:P * c + P], ident[:])
                last.then_inc(xT2_psum, 1)

            def project_t(b, w, done):
                for d in range(CC):
                    for c in range(CC):
                        last = m.matmul(bank[6][:, T * d:T * d + T], w[:, c, P * d:P * d + P], xT2[:, c, :],
                                        start=(c == 0), stop=(c == CC - 1))
                last.then_inc(done, 1)

            def q_job(b):
                pe.wait_ge(xT2_ready, b + 1)
                need(pe, rel_ready, b)
                project_t(b, wq, q_psum)

            def k_job(b):
                pe.wait_ge(q_ready, b + 1)
                project_t(b, wk, k_psum)

            def v_job(b):
                pe.wait_ge(k_ready, b + 1)
                for t in range(2):
                    for c in range(CC):
                        last = m.matmul(bank[6][:, C * t:C * t + C], xT2[:, c, P * t:P * t + P], wv[:, c, :],
                                        start=(c == 0), stop=(c == CC - 1))
                last.then_inc(v_psum, 1)

            def raw_job(b, u):
                pe.wait_ge(sigma_ready, b + 1)
                need(pe, mem_used, 4 * b)
                if isinstance(b, int) and b == 0:
                    pe.wait_ge(v_ready, 1)
                for t in range(2):
                    for c in range(CC):
                        last = m.matmul(bank[6][:, MEM * t:MEM * t + MEM], sigma[u][:, c, P * t:P * t + P], nrm[:, c, :],
                                        start=(c == 0), stop=(c == CC - 1))
                last.then_inc(raw_psum, 1)

            def rel_job(b):
                pe.wait_ge(raw_ready, b + 1)
                for t in range(2):
                    last = m.matmul(bank[6][:, 16:16 + MEM], mean_w[:], raw[:, t, :], start=(t == 0), stop=(t == 1))
                last.then_inc(rel_psum, 1)

            def mem_job(b, u, j, last_batch):
                if j == 0:
                    need(pe, wo_used, b)
                if j == 1:
                    pe.wait_ge(rel_ready, b + 1)
                    pe.wait_ge(v_ready, b + 1 if last_batch else b + 2)
                if j >= 2:
                    pe.wait_ge(mem_used, 4 * b + j - 1)
                for c in range(CC):
                    last = m.matmul(bank[6 + (7 + j) % 2][:], sigma[u][:, c, P * (j // 2):P * (j // 2) + P],
                                    mems[:, c, 512 * (j % 2):512 * (j % 2) + 512], start=(c == 0), stop=(c == CC - 1))
                last.then_inc(mem_psum, 1)

            def mix_job(b, last_batch):
                pe.wait_ge(mix_ready, b + 1)
                if not last_batch:
                    pe.wait_ge(xT2_ready, b + 3)
                for c in range(CC):
                    for t in range(2):
                        last = m.transpose(bank[7][:, T * c + P * t:T * c + P * t + P], mix[:, t, P * c:P * c + P], ident[:])
                last.then_inc(mixT_psum, 1)

            def out_job(b):
                pe.wait_ge(mixT_ready, b + 1)
                for t in range(2):
                    for c in range(CC):
                        last = m.matmul(bank[7][:, C * t:C * t + C], mixT[:, c, P * t:P * t + P], wo[:, c, :],
                                        start=(c == 0), stop=(c == CC - 1))
                last.then_inc(wo_psum, 1)

            def body(b, u, first=False, last=False):
                for n in range(UNITS):
                    U = UNITS * b + n
                    scores(b, u, n)
                    if n == 0:
                        raw_job(b, u)
                    if n == 1:
                        rel_job(b)
                    if not last:
                        {1: turn_x, 2: q_job, 4: k_job, 6: v_job}.get(n, lambda b: None)(b + 1)
                    if n == 3 and not first:
                        mix_job(b - 1, last)
                    if n == 5 and not first:
                        out_job(b - 1)
                    if 7 <= n < 11:
                        mem_job(b, u, n - 7, last)
                    if n or not first:
                        turn_p(U - 1, (n - 1) % UNITS)
                    if n >= 2:
                        values(b, u, n - 2)
                    elif not first:
                        values(b - 1, 1 - u, n + UNITS - 2)

            def attention_():
                pe.wait_ge(aw_loaded, 112)
                turn_x(0)
                q_job(0)
                k_job(0)
                v_job(0)
                body(0, 0, first=True)
                with pe.Fori(0, B // 2 - 1) as i:
                    body(2 * i + 1, 1)
                    body(2 * i + 2, 0)
                body(B - 1, 1, last=True)
                turn_p(UNITS * B - 1, UNITS - 1)
                values(B - 1, 1, UNITS - 2)
                values(B - 1, 1, UNITS - 1)
                mix_job(B - 1, True)
                out_job(B - 1)

            for f in range(layers):
                moe(f)
                if attention and f == 0:
                    attention_()


def kernel(L0_attn_x, L0_attn_w_q, L0_attn_w_k, L0_attn_w_v, L0_attn_w_o, L0_attn_gate, L0_attn_memories,
           L0_attn_memory_norms, L0_ffn_w_gate, L0_ffn_w_shared_up, L0_ffn_w_shared_down, L0_ffn_w_up, L0_ffn_w_down):
    import numpy as np
    import concourse.bacc as bacc
    from concourse.bass_utils import run_bass_kernel_spmd

    def chunked(w):
        return w.reshape(CC, P, -1).transpose(1, 0, 2)

    arrays = {
        "x": np.asarray(L0_attn_x).reshape(N, C),
        "w_tok": chunked(np.concatenate([np.asarray(L0_ffn_w_shared_up), np.asarray(L0_ffn_w_gate)], axis=1)),
        "w_shared_down": np.asarray(L0_ffn_w_shared_down),
        "w_up": np.asarray(L0_ffn_w_up).reshape(E, CC, P, 2 * H).transpose(2, 1, 0, 3),
        "w_down": np.asarray(L0_ffn_w_down).reshape(NG, P, C).transpose(1, 0, 2),
        "w_q": chunked(np.asarray(L0_attn_w_q).T),
        "w_k": chunked(np.asarray(L0_attn_w_k).T),
        "w_v": chunked(np.asarray(L0_attn_w_v).T),
        "w_o": chunked(np.asarray(L0_attn_w_o).T),
        "memories": chunked(np.asarray(L0_attn_memories).transpose(1, 0, 2).reshape(C, MEM * C)),
        "norms": chunked(np.asarray(L0_attn_memory_norms).T),
        "gate": np.asarray(L0_attn_gate).reshape(1, 1),
    }
    arrays = {k: np.ascontiguousarray(a) for k, a in arrays.items()}
    nc = bacc.Bacc("TRN2", target_bir_lowering=False, num_devices=1)
    args = [nc.dram_tensor(k, a.shape, F32, kind="ExternalInput").ap() for k, a in arrays.items()]
    out = nc.dram_tensor("out", (N, C), F32, kind="ExternalOutput").ap()
    table = nc.dram_tensor("table", (TABLE, ROW), F32, kind="Internal").ap()
    acc = [nc.dram_tensor(f"acc{r}", (DUMP, C), F32, kind="Internal").ap() for r in range(2)]
    thirds = nc.dram_tensor("thirds", (2, 2, 3, C, T), BF16, kind="Internal").ap()
    program(nc, *args, thirds, out, table, acc)
    r = run_bass_kernel_spmd(nc, [arrays], core_ids=[0])
    return r.results[0]["out"].reshape(B, T, C)
```

```python
from contextlib import ExitStack, contextmanager

import concourse.bass as bass
from concourse import mybir

F32 = mybir.dt.float32
BF16 = mybir.dt.bfloat16
U32 = mybir.dt.uint32
ALU = mybir.AluOpType
ACT = mybir.ActivationFunctionType
AX = mybir.AxisListType

LAYERS = 2
P = 128
B, T, C = 8, 256, 256
N = B * T
NT = N // P
CC = C // P
E, H, HS = 64, 32, 64
TOPK, CAP = 6, 128
EG = 4
NG = E // EG
META = E + 1
ROW = C + META
SLOTS = E * CAP
TABLE = SLOTS + TOPK * N
DUMP = N + P
HALF = NT // 2
ACCS = EG
PARTS = ((0, 2), (2, 6), (6, 10), (10, 14), (14, NT))
EARLY = NT - 2
FIRST = (0, EARLY)
SHIFT = NT - EARLY
CHOSEN0 = (1, NT + 2 + EARLY // 2 - EARLY)
LN_EPS = 1e-5
NHEAD = 16
HD = C // NHEAD
MEM = 4
QUAD = 32
CLIP = 1e-6
UNITS = 12
Q_SLOTS = (0, 0, 1, 1, 0, 2)
K_SLOTS = (0, 1, 0, 1, 2, 0)
STACK = HD * len(Q_SLOTS)


def need(eng, sem, count):
    if not (isinstance(count, int) and count <= 0):
        eng.wait_ge(sem, count)


class Own:

    def __init__(self, eng, sem):
        self.eng, self.sem, self.base, self.n = eng, sem, 0, 0

    def mark(self, ins):
        ins.then_inc(self.sem, 1)
        self.n += 1

    def settle(self):
        self.eng.wait_ge(self.sem, self.base + self.n)

    def link(self, ins):
        self.mark(ins)
        self.settle()

    @contextmanager
    def loop(self, start, end, per):
        total = self.base + self.n
        with self.eng.Fori(start, end) as i:
            self.base, self.n = i * per + (total - start * per), 0
            yield i
            assert self.n == per, (self.n, per)
        self.base, self.n = total + (end - start) * per, 0


def program(nc, x_in, w_tok, w_shared_down, w_up, w_down, w_q, w_k, w_v, w_o, memories, norms, gate, thirds, out, table, acc):
    ctx = ExitStack()
    with ctx:
        def sb(name, shape, dt=F32):
            return ctx.enter_context(nc.sbuf_tensor(name, shape, dt))

        def sem(name):
            return ctx.enter_context(nc.semaphore(name))

        bank = [ctx.enter_context(nc.psum_tensor(f"bank{i}", [P, 512], F32)) for i in range(8)]

        ident = sb("ident", [P, P])
        identb = sb("identb", [P, P], BF16)
        before = sb("before", [P, P], BF16)
        ones = sb("ones", [P, P], BF16)
        expert_no = sb("expert_no", [P, E])
        slot_end = sb("slot_end", [P, E])
        over_row = sb("over_row", [P, NT * TOPK])
        zrow = sb("zrow", [P, ROW])
        minus_half = sb("minus_half", [P, NT])
        wtok = sb("wtok", [P, CC, 2 * HS + E])
        wsd = sb("wsd", [HS, C])
        wup = sb("wup", [P, CC, E, 2 * H])
        wdn = sb("wdn", [P, NG, C])
        X = sb("X", [P, NT, C])
        st = sb("st", [P, NT, 6])
        mean = sb("mean", [P, NT])
        dev = sb("dev", [P, NT])
        ve = sb("ve", [P, NT])
        rstd = sb("rstd", [P, NT])
        rows = sb("rows", [P, NT, ROW])
        xT = sb("xT", [P, 2, CC * P])
        en = sb("en", [P, 2, E])
        tg = sb("tg", [P, 2, HS])
        sg = sb("sg", [P, 2, E + 2])
        sh1 = sb("sh1", [P, HS])
        sh = sb("sh", [P, 2, HS])
        shT = sb("shT", [HS, 2, P])
        top8 = sb("top8", [P, 8])
        rep = sb("rep", [P, E + 2])
        ssum = sb("ssum", [P, 3])
        mask = sb("mask", [P, 2, E], BF16)
        chosen = sb("chosen", [P, E], BF16)
        end_of = sb("end_of", [P, 2, E])
        fits = sb("fits", [P, E])
        key = sb("key", [P, E])
        key8 = sb("key8", [P, 8])
        over = sb("over", [P, TOPK])
        sh1p = sb("sh1p", [P, 2, HS])
        top8p = sb("top8p", [P, 2, 8])
        repp = sb("repp", [P, 2, E + 2])
        ssump = sb("ssump", [P, 3, 2])
        fitsp = sb("fitsp", [P, 2, E])
        keyp = sb("keyp", [P, 2, E])
        key8p = sb("key8p", [P, 2, 8])
        overp = sb("overp", [P, 2, TOPK])
        slot = sb("slot", [P, NT, TOPK], U32)
        IDX = sb("IDX", [P, E], U32)
        xg = [sb(f"xg{u}", [P, EG, ROW]) for u in range(2)]
        meta = [sb(f"meta{u}", [P, EG, META]) for u in range(2)]
        xdT_both = sb("xdT", [P, 2, CC, EG * P])
        xdT = [xdT_both[:, u] for u in range(2)]
        eg = [sb(f"eg{u}", [P, EG, H]) for u in range(2)]
        hbig = [sb(f"hbig{u}", [P, EG * P]) for u in range(2)]
        hT = [sb(f"hT{u}", [P, EG * P]) for u in range(2)]
        ysb_both = sb("ysb", [P, 2, EG, C])
        ysb = [ysb_both[:, u] for u in range(2)]
        fin2, fin3 = ([m.rearrange("p (t c) -> p t c", c=C) for m in
                       (flat[:, 0:4 * C], flat[:, 4 * C:8 * C])] for flat in
                      (ysb_both[:].rearrange("p u e c -> p (u e c)"), xdT_both[:].rearrange("p u c s -> p (u c s)")))
        fin = rows[:].rearrange("p t c -> p (t c)")[:, 0:NT * C].rearrange("p (t c) -> p t c", c=C)

        rowp = [xg[u][:, 0:2, :] for u in range(2)]
        pj = xg[0][:, 2:4, 0:2 * HS + E]

        wq, wk, wv, wo = (sb(n, [P, CC, C]) for n in ("wq", "wk", "wv", "wo"))
        mems = sb("mems", [P, CC, MEM * C])
        nrm = sb("nrm", [P, CC, MEM])
        gt = sb("gt", [P, 4])
        mean_w = sb("mean_w", [P, P])
        causal = sb("causal", [P, 4, P], BF16)
        xn = sb("xn", [P, 2, C])
        xT2 = sb("xT2", [P, CC, T])
        qT = sb("qT", [P, CC * T])
        kT = sb("kT", [P, CC * T])
        rest = [sb(f"rest{w}", [P, CC * T]) for w in range(2)]
        part = [sb(f"part{w}", [P, 3, CC * T], BF16) for w in range(2)]
        def stacks(ap, count):
            flat = ap.bitcast(BF16).rearrange("p (u h t) -> p u h t", u=count, h=NHEAD)
            return [flat[0:STACK, u] for u in range(count)]

        QS = stacks(rows[:].rearrange("p t c -> p (t c)")[:, 0:NT * C], 2)
        KS = stacks(ysb_both[:].rearrange("p u e c -> p (u e c)"), 1) + \
            stacks(xdT_both[:].rearrange("p u c s -> p (u c s)"), 1)
        V = [sb(f"V{u}", [P, 2, NHEAD, QUAD]) for u in range(2)]
        OT = sb("OT", [P, 2, 4 * P])
        sigma = [sb(f"sigma{u}", [P, CC, T]) for u in range(2)]
        raw = sb("raw", [P, 2, MEM])
        rawc = sb("rawc", [P, 2, MEM])
        rel = sb("rel", [P, MEM])
        wm = sb("wm", [P, 2 * MEM])
        wsc = sb("wsc", [P, 4])
        coef = sb("coef", [P, 2, MEM])
        memo = sb("memo", [P, 2, C])
        negmax = [sb(f"negmax{u}", [P, 4]) for u in range(2)]
        Pr = [sb(f"Pr{u}", [P, 512]) for u in range(2)]
        PT = [sb(f"PT{u}", [P, 512]) for u in range(2)]
        rl = sb("rl", [P, 2, NHEAD])
        mix = sb("mix", [P, 2, C])
        mixT = sb("mixT", [P, CC, T])

        x_loaded, tok_loaded, w_loaded = sem("x_loaded"), sem("tok_loaded"), sem("w_loaded")
        const_set, const_ready = sem("const_set"), sem("const_ready")
        dve_own = sem("dve_own")
        var_ready, rstd_ready = sem("var_ready"), sem("rstd_ready")
        xn_ready, xT_psum, xT_ready, proj_ready, e_ready, tg_ready = (
            sem("xn_ready"), sem("xT_psum"), sem("xT_ready"), sem("proj_ready"), sem("e_ready"), sem("tg_ready"))
        sh_ready, mask_ready, weights_ready = sem("sh_ready"), sem("mask_ready"), sem("weights_ready")
        empty_set, table_set, ids_set = sem("empty_set"), sem("table_set"), sem("ids_set")
        chosen_ready, slot_psum, slot_ready, shT_psum, shT_ready = (
            sem("chosen_ready"), sem("slot_psum"), sem("slot_ready"), sem("shT_psum"), sem("shT_ready"))
        shd_psum, x_shared = sem("shd_psum"), sem("x_shared")
        row_ready, dispatched, meta_ready, idx_ready = sem("row_ready"), sem("dispatched"), sem("meta_ready"), sem("idx_ready")
        slots_loaded = [sem("slots_loaded0"), sem("slots_loaded1")]
        t0_psum, t1_psum, xd0_ready, xd1_ready = (
            sem("t0_psum"), sem("t1_psum"), sem("xd0_ready"), sem("xd1_ready"))
        up_psum, eg_ready, h_ready, hT_psum, hT_ready = (
            sem("up_psum"), sem("eg_ready"), sem("h_ready"), sem("hT_psum"), sem("hT_ready"))
        y_psum, ya_ready, yb_ready = sem("y_psum"), sem("ya_ready"), sem("yb_ready")
        acc_set = [sem(f"acc_set{r}") for r in range(ACCS)]
        acc_done = [sem(f"acc_done{r}") for r in range(ACCS)]
        fin_loaded = [sem(f"fin_loaded{c}") for c in range(len(PARTS))]
        summed, stored = sem("summed"), sem("stored")
        aw_loaded, gate_exp = sem("aw_loaded"), sem("gate_exp")
        xn2_ready, xT2_psum, xT2_ready = sem("xn2_ready"), sem("xT2_psum"), sem("xT2_ready")
        q_psum, q_ready, k_psum, k_ready, v_psum, v_ready = (
            sem("q_psum"), sem("q_ready"), sem("k_psum"), sem("k_ready"), sem("v_psum"), sem("v_ready"))
        expq_ready, sigma_ready = sem("expq_ready"), sem("sigma_ready")
        pool_own = sem("pool_own")
        thirds_ready, thirds_stored = sem("thirds_ready"), [sem("q_thirds_stored"), sem("k_thirds_stored")]
        stacked = [sem("stacked0"), sem("stacked1")]
        raw_psum, raw_ready, rel_psum, rel_ready, wm_ready = (
            sem("raw_psum"), sem("raw_ready"), sem("rel_psum"), sem("rel_ready"), sem("wm_ready"))
        mem_psum, mem_used = sem("mem_psum"), sem("mem_used")
        s_psum, max_ready, p_ready, pt_psum, pt_ready, pv_done = (
            sem("s_psum"), sem("max_ready"), sem("p_ready"), sem("pt_psum"), sem("pt_ready"), sem("pv_done"))
        pair_xn, pair_xT_psum, pair_xT, pair_proj_psum, pair_proj = (
            sem("pair_xn"), sem("pair_xT_psum"), sem("pair_xT"), sem("pair_proj_psum"), sem("pair_proj"))
        pair_sh, pair_mask, pair_weights, pair_ids = (
            sem("pair_sh"), sem("pair_mask"), sem("pair_weights"), sem("pair_ids"))
        pair_slot_psum, pair_slot_used, pair_slot, pair_shT, pair_shd_psum, pair_added = (
            sem("pair_slot_psum"), sem("pair_slot_used"), sem("pair_slot"), sem("pair_shT"), sem("pair_shd_psum"),
            sem("pair_added"))
        OT_ready, o_turned, o_used = sem("OT_ready"), sem("o_turned"), sem("o_used")
        mix_ready, mixT_psum, mixT_ready, wo_psum, wo_used = (
            sem("mix_ready"), sem("mixT_psum"), sem("mixT_ready"), sem("wo_psum"), sem("wo_used"))

        ZPARTS = NT // 4 + 1
        SET0 = (16 * NT, 16 * (NT + EARLY // 2 + NT - EARLY))
        ADDS = 16 * NG

        block = ctx.enter_context(nc.Block())

        @block.sync
        def _(sp):
            x_t = x_in.rearrange("(t p) c -> p t c", p=P)
            out_t = out.rearrange("(t p) c -> p t c", p=P)
            slots_t = table[0:SLOTS, :].rearrange("(e p) c -> p e c", p=P)
            empty = zrow[:].rearrange("p (o c) -> p o c", o=1)
            acc_t = [a[0:N, :].rearrange("(t p) c -> p t c", p=P) for a in acc]
            sp.dma_start(X[:], x_t).then_inc(x_loaded, 16)
            sp.dma_start(wtok[:], w_tok).then_inc(tok_loaded, 16)
            sp.dma_start(wsd[:], w_shared_down).then_inc(tok_loaded, 16)
            sp.wait_ge(empty_set, 2)
            for c in range(8):
                sp.dma_start(slots_t[:, 8 * c:8 * c + 8, :], empty.to_broadcast([P, 8, ROW])).then_inc(table_set, 16)
            sp.dma_start(wup[:], w_up).then_inc(w_loaded, 16)
            sp.dma_start(wdn[:], w_down).then_inc(w_loaded, 16)
            for w, src in ((wq, w_q), (wk, w_k), (wv, w_v), (wo, w_o), (mems, memories), (nrm, norms)):
                sp.dma_start(w[:], src).then_inc(aw_loaded, 16)
            sp.dma_start(gt[:, 0:1], gate.to_broadcast([P, 1])).then_inc(aw_loaded, 16)

            def clear():
                zeros = zrow[:, 0:C].rearrange("p (o c) -> p o c", o=1)
                for r in range(1, ACCS):
                    for c in range(ZPARTS):
                        part_ = acc[r][4 * P * c:min(4 * P * (c + 1), DUMP), :].rearrange("(t p) c -> p t c", p=P)
                        sp.dma_start(part_, zeros.to_broadcast(list(part_.shape))).then_inc(acc_set[r], 16)

            def moe(f):
                if not f:
                    clear()
                    sp.dma_start(acc[0][N:DUMP, :], zrow[:, 0:C]).then_inc(w_loaded, 16)

                with sp.Fori(FIRST[f], NT) as t:
                    sp.wait_ge(x_shared, t + SHIFT * f + 1)
                    sp.dma_start(acc_t[0][:, bass.ds(t, 1), :], X[:, bass.ds(t, 1), :]).then_inc(acc_set[0], 16)

                def load_group(i, u):
                    sp.dma_start(xg[u][:], slots_t[:, bass.ds(EG * (2 * i + u), EG), :]).then_inc(slots_loaded[u], 16)

                sp.wait_ge(dispatched, 16 * TOPK * NT * (f + 1))
                load_group(0, 0)
                load_group(0, 1)
                with sp.Fori(1, NG // 2) as i:
                    for u in range(2):
                        sp.wait_ge(t1_psum, 2 * i + (u - 1 + NG * f))
                        sp.wait_ge(meta_ready, 2 * i + (u - 1 + NG * f))
                        load_group(i, u)
                for r in range(ACCS):
                    sp.wait_ge(acc_done[r], ADDS * (f + 1))
                for c, (t0, t1) in enumerate(PARTS):
                    tiles = slice(t0, t1)
                    sp.dma_start(X[:, tiles, :], acc_t[0][:, tiles, :]).then_inc(fin_loaded[c], 16)
                    sp.dma_start(fin[:, tiles, :], acc_t[1][:, tiles, :]).then_inc(fin_loaded[c], 16)
                    if c >= 2:
                        sp.wait_ge(summed, len(PARTS) * f + c - 1)
                    for src, dst in ((acc_t[2], fin2), (acc_t[3], fin3)):
                        sp.dma_start(dst[c % 2][:, 0:t1 - t0, :], src[:, tiles, :]).then_inc(fin_loaded[c], 16)

            def store_thirds(b, u, w):
                sp.wait_ge(thirds_ready, 2 * b + w + 1)
                if b >= 2:
                    sp.wait_ge(stacked[u], (b - u) * (8 * 2 * len(Q_SLOTS)))
                for k in range(3):
                    sp.dma_start(thirds[u, w, k].rearrange("(c p) t -> p c t", p=P),
                                 part[w][:, k, :].rearrange("p (c t) -> p c t", c=CC)).then_inc(thirds_stored[w], 16)

            def load_stack(b, u, w):
                sp.wait_ge(thirds_stored[w], (b + 1) * 48)
                if b >= 2:
                    sp.wait_ge(s_psum, (b - 1) * UNITS)
                dst, slots = ((QS, Q_SLOTS), (KS, K_SLOTS))[w]
                for s_, k in enumerate(slots):
                    sp.dma_start(dst[u][HD * s_:HD * s_ + HD, :, :],
                                 thirds[u, w, k].rearrange("(h d) t -> d h t", d=HD)).then_inc(stacked[u], 16)

            def attention_():
                def store_pair(c):
                    sp.wait_ge(pair_added, c + 1)
                    sp.dma_start(acc_t[0][:, 2 * c:2 * c + 2, :], X[:, 2 * c:2 * c + 2, :]).then_inc(acc_set[0], 16)

                for b in range(B):
                    if b:
                        for w in range(2):
                            store_thirds(b, b % 2, w)
                            load_stack(b, b % 2, w)
                    else:
                        store_thirds(0, 0, 0)
                        store_thirds(0, 0, 1)
                        sp.wait_ge(summed, len(PARTS))
                        load_stack(0, 0, 0)
                        load_stack(0, 0, 1)
                    if b == 2:
                        clear()
                    if b >= 3:
                        store_pair(b - 3)
                    if b == 1:
                        for c in range(8):
                            sp.dma_start(slots_t[:, 8 * c:8 * c + 8, C:],
                                         empty[:, :, C:].to_broadcast([P, 8, META])).then_inc(table_set, 16)
                store_pair(EARLY // 2 - 2)
                store_pair(EARLY // 2 - 1)

            for f in range(LAYERS):
                moe(f)
                if f == 0:
                    attention_()
            for c, (t0, t1) in enumerate(PARTS):
                sp.wait_ge(summed, len(PARTS) * (LAYERS - 1) + c + 1)
                sp.dma_start(out_t[:, t0:t1, :], X[:, t0:t1, :]).then_inc(stored, 16)
            sp.wait_ge(stored, 16 * len(PARTS))

        @block.gpsimd
        def _(pool):
            g = nc.gpsimd
            g.memset(zrow[:, 0:ROW - 1], 0.0).then_inc(empty_set, 1)
            g.iota(zrow[:, ROW - 1:ROW], [[0, 1]], base=N, channel_multiplier=1,
                   allow_small_or_imprecise_dtypes=True).then_inc(empty_set, 1)
            g.memset(causal[:], 0.0).then_inc(pool_own, 1)
            g.memset(mean_w[:], 1.0 / T).then_inc(const_ready, 1)
            for u in range(2):
                g.memset(V[u][:, :, :, HD:HD + 1], 1.0).then_inc(const_ready, 1)
                g.memset(V[u][:, :, :, HD + 1:], 0.0).then_inc(const_ready, 1)
            for m in (ident, identb, hbig[0], hbig[1]):
                g.memset(m[:], 0.0).then_inc(const_set, 1)
            g.memset(minus_half[:], -0.5).then_inc(const_set, 1)
            g.memset(before[:], 1.0).then_inc(const_set, 1)
            g.memset(ones[:], 1.0).then_inc(const_set, 1)
            for m, step, base in ((expert_no, 1, 0), (slot_end, CAP, CAP)):
                g.iota(m[:], [[step, E]], base=base, channel_multiplier=0,
                       allow_small_or_imprecise_dtypes=True).then_inc(const_set, 1)
            g.iota(over_row[:], [[P, NT * TOPK]], base=SLOTS + 1, channel_multiplier=1,
                   allow_small_or_imprecise_dtypes=True).then_inc(const_set, 1)
            pool.wait_ge(const_set, 10)
            g.affine_select(out=before[:], in_=before[:], compare_op=ALU.is_gt, fill=0.0, base=0,
                            pattern=[[1, P]], channel_multiplier=-1).then_inc(const_ready, 1)
            for m in (ident, identb):
                g.affine_select(out=m[:], in_=m[:], compare_op=ALU.not_equal, fill=1.0, base=0,
                                pattern=[[-1, P]], channel_multiplier=1).then_inc(const_ready, 1)
            pool.wait_ge(pool_own, 1)
            g.affine_select(out=causal[:], in_=causal[:], compare_op=ALU.is_ge, fill=-1e9, base=0,
                            pattern=[[0, 4], [-1, P]], channel_multiplier=1).then_inc(const_ready, 1)

            computed = [0]

            def reciprocal_deviations(t0, t1):
                computed[0] += 1
                pool.wait_ge(var_ready, computed[0])
                g.tensor_tensor(rstd[:, t0:t1], ve[:, t0:t1], minus_half[:, t0:t1], ALU.pow).then_inc(rstd_ready, 1)

            def scatter(t, rows_):
                for k in range(TOPK):
                    g.indirect_dma_start(out=table[:, :], out_offset=bass.IndirectOffsetOnAxis(slot[:, t, k:k + 1], 0),
                                         in_=rows_, in_offset=None).then_inc(dispatched, 16)

            def moe(f):
                if not f:
                    reciprocal_deviations(0, NT)
                g.iota(rows[:, :, ROW - 1], [[P, NT]], base=0, channel_multiplier=1,
                       allow_small_or_imprecise_dtypes=True).then_inc(ids_set, 1)
                pool.wait_ge(ids_set, f + 1)
                pool.wait_ge(table_set, 128 * (f + 1))

                for t in range(FIRST[f], NT):
                    s = t + 1 + SHIFT * f
                    pool.wait_ge(row_ready, s)
                    pool.wait_ge(weights_ready, s)
                    pool.wait_ge(slot_ready, s)
                    scatter(t, rows[:, t, :])

                for r in range(ACCS):
                    pool.wait_ge(acc_set[r], 16 * ZPARTS * (f + 1) if r else SET0[f])
                for n in range(E):
                    gi, e = n // EG, n % EG
                    if e == 0:
                        pool.wait_ge(idx_ready, gi + NG * f + 1)
                        pool.wait_ge(ya_ready, gi + NG * f + 1)
                    if e == 2:
                        pool.wait_ge(yb_ready, gi + NG * f + 1)
                    if gi > 0:
                        pool.wait_ge(acc_done[e], 16 * gi + ADDS * f)
                    g.indirect_dma_start(out=acc[e][:, :], out_offset=bass.IndirectOffsetOnAxis(IDX[:, n:n + 1], 0),
                                         in_=ysb[gi % 2][:, e, :], in_offset=None, compute_op=ALU.add)\
                     .then_inc(acc_done[e], 16)

            def thirds_of(src, ready, w, b):
                pool.wait_ge(ready, 2 * b + 2)
                if not (isinstance(b, int) and b == 0):
                    pool.wait_ge(thirds_stored[w], b * 48)
                base = 6 * b + 3 * w
                g.tensor_tensor(rest[w][:], src[:], part[w][:, 0, :], ALU.subtract).then_inc(pool_own, 1)
                pool.wait_ge(pool_own, base + 2)
                g.tensor_copy(part[w][:, 1, :], rest[w][:]).then_inc(pool_own, 1)
                pool.wait_ge(pool_own, base + 3)
                g.tensor_tensor(rest[w][:], rest[w][:], part[w][:, 1, :], ALU.subtract).then_inc(pool_own, 1)
                pool.wait_ge(pool_own, base + 4)
                g.tensor_copy(part[w][:, 2, :], rest[w][:]).then_inc(thirds_ready, 1)

            def attention_():
                reciprocal_deviations(*PARTS[0])
                number_pair(0)
                for b in range(B + 1):
                    if b < B:
                        thirds_of(qT, q_ready, 0, b)
                        thirds_of(kT, k_ready, 1, b)
                    if b == 0:
                        reciprocal_deviations(PARTS[0][1], NT)
                    if b >= 2:
                        reciprocal_deviations(2 * (b - 2), 2 * (b - 2) + 2)
                    if b >= 3:
                        dispatch_pair(b - 3)
                reciprocal_deviations(NT - 2, NT)
                dispatch_pair(EARLY // 2 - 1)

            def number_pair(c):
                if c >= 2:
                    pool.wait_ge(dispatched, 16 * TOPK * (NT + 2 * (c - 1)))
                g.iota(rowp[c % 2][:, :, ROW - 1], [[P, 2]], base=2 * P * c, channel_multiplier=1,
                       allow_small_or_imprecise_dtypes=True).then_inc(pair_ids, 1)

            def dispatch_pair(c):
                if c + 1 < EARLY // 2:
                    number_pair(c + 1)
                pool.wait_ge(pair_ids, c + 1)
                pool.wait_ge(pair_xn, 2 * c + 2)
                pool.wait_ge(pair_weights, 2 * c + 2)
                pool.wait_ge(pair_slot, c + 1)
                pool.wait_ge(table_set, 256)
                for t in range(2):
                    scatter(2 * c + t, rowp[c % 2][:, t, :])

            for f in range(LAYERS):
                moe(f)
                if f == 0:
                    attention_()

        @block.scalar
        def _(act):
            a = nc.scalar

            def moe(f):
                def copy_xT(i, u):
                    s = 2 * i + u + SHIFT * f
                    act.wait_ge(xn_ready, s + 1)
                    a.activation(rows[:, bass.ds(2 * i + u, 1), 0:C].rearrange("p o c -> p (o c)"), xn[:, u, :], ACT.Copy)\
                     .then_inc(row_ready, 1)
                    act.wait_ge(xT_psum, s + 1)
                    a.activation(xT[:, u, :], bank[u][:, 0:CC * P], ACT.Copy).then_inc(xT_ready, 1)

                def exp_gates(i, u):
                    s = 2 * i + u + SHIFT * f
                    act.wait_ge(proj_ready, s + 1)
                    a.activation(en[:, u, :], bank[2 + u][:, 2 * HS:2 * HS + E], ACT.Exp, scale=-1.0).then_inc(e_ready, 1)
                    a.activation(tg[:, u, :], bank[2 + u][:, HS:2 * HS], ACT.Tanh, scale=0.5).then_inc(tg_ready, 1)

                def copy_shT(i, u):
                    s = 2 * i + u + SHIFT * f
                    act.wait_ge(shT_psum, s + 1)
                    a.activation(shT[:, u, :], bank[5][0:HS, 0:P], ACT.Copy).then_inc(shT_ready, 1)

                def step(i, u, last=False):
                    if not last:
                        copy_xT(i + u, 1 - u)
                        exp_gates(i + u, 1 - u)
                    copy_shT(i, u)

                i0 = FIRST[f] // 2
                copy_xT(i0, 0)
                exp_gates(i0, 0)
                if i0 < HALF - 1:
                    with act.Fori(i0, HALF - 1) as i:
                        step(i, 0)
                        step(i, 1)
                step(HALF - 1, 0)
                step(HALF - 1, 1, last=True)

                def copy_xd(i, u):
                    act.wait_ge(slots_loaded[u], i * 16 + 16 * (NG // 2 * f + 1))
                    if not (isinstance(i, int) and 2 * i + u < 2 and not f):
                        act.wait_ge(h_ready, 2 * i + u + NG * f - 1)
                    a.activation(meta[u][:], xg[u][:, :, C:ROW], ACT.Copy).then_inc(meta_ready, 1)
                    act.wait_ge(t0_psum, 2 * i + u + NG * f + 1)
                    a.activation(xdT[u][:, 0, :], bank[0][:], ACT.Copy).then_inc(xd0_ready, 1)

                def copy_hT(i, u):
                    act.wait_ge(hT_psum, 2 * i + u + NG * f + 1)
                    a.activation(hT[u][:], bank[4][:], ACT.Copy).then_inc(hT_ready, 1)

                def tanh_up(i, u):
                    act.wait_ge(up_psum, 2 * i + u + NG * f + 1)
                    v = bank[2 + u][:, 0:EG * 2 * H].rearrange("p (e h) -> p e h", e=EG)
                    a.activation(eg[u][:], v[:, :, 0:H], ACT.Tanh, scale=0.5).then_inc(eg_ready, 1)

                def copy_y(i, u):
                    act.wait_ge(y_psum, 2 * i + u + NG * f + 1)
                    if not (isinstance(i, int) and i == 0):
                        act.wait_ge(acc_done[0], i * 32 + (16 * u - 16 + ADDS * f))
                        act.wait_ge(acc_done[1], i * 32 + (16 * u - 16 + ADDS * f))
                    a.activation(ysb[u][:, 0:2, :], bank[5][:].rearrange("p (e c) -> p e c", e=2), ACT.Copy)\
                     .then_inc(ya_ready, 1)

                def estep(i, u, rows_=True, ups=True):
                    if rows_:
                        copy_xd(i + 1 + u, 1 - u)
                    copy_hT(i, u)
                    if ups:
                        tanh_up(i + 1, u)
                    copy_y(i, u)

                copy_xd(0, 0)
                copy_xd(0, 1)
                tanh_up(0, 0)
                copy_xd(1, 0)
                tanh_up(0, 1)
                estep(0, 0)
                estep(0, 1)
                estep(1, 0)
                with act.Fori(1, NG // 2 - 2) as i:
                    estep(i, 1)
                    estep(i + 1, 0)
                estep(NG // 2 - 2, 1, rows_=False)
                estep(NG // 2 - 1, 0, rows_=False, ups=False)
                estep(NG // 2 - 1, 1, rows_=False, ups=False)

            def exps(b, u, n):
                U = UNITS * b + n
                need(act, max_ready, U + 1)
                need(act, pt_psum, U - 1)
                k = 4 if n % 3 == 0 else 2
                w = 512 // k
                for i in range(k):
                    last = a.activation(Pr[n % 2][:, w * i:w * i + w], bank[n % 2][:, w * i:w * i + w], ACT.Exp,
                                        bias=negmax[n % 2][:, i:i + 1])
                last.then_inc(p_ready, 1)

            def copy_qT(b, u):
                act.wait_ge(q_psum, b + 1)
                need(act, thirds_ready, 2 * b - 1)
                need(act, sigma_ready, b)
                need(act, thirds_stored[0], 48 * b)
                a.activation(qT[:], bank[6][:], ACT.Copy).then_inc(q_ready, 1)
                a.activation(part[0][:, 0, :], bank[6][:], ACT.Copy).then_inc(q_ready, 1)
                act.wait_ge(q_ready, 2 * b + 2)
                a.activation(sigma[u][:].rearrange("p c t -> p (c t)"), qT[:], ACT.Exp).then_inc(expq_ready, 1)

            def copy_kT(b):
                act.wait_ge(k_psum, b + 1)
                need(act, thirds_ready, 2 * b)
                need(act, thirds_stored[1], 48 * b)
                a.activation(kT[:], bank[6][:], ACT.Copy, scale=HD ** -0.5).then_inc(k_ready, 1)
                a.activation(part[1][:, 0, :], bank[6][:], ACT.Copy, scale=HD ** -0.5).then_inc(k_ready, 1)

            def copy_xT2(b):
                act.wait_ge(xT2_psum, b + 1)
                a.activation(xT2[:].rearrange("p c t -> p (c t)"), bank[7][:], ACT.Copy).then_inc(xT2_ready, 1)

            def copy_v(b, u):
                act.wait_ge(v_psum, b + 1)
                a.activation(V[u][:, :, :, 0:HD], bank[6][:].rearrange("p (t h d) -> p t h d", t=2, h=NHEAD), ACT.Copy)\
                 .then_inc(v_ready, 1)

            def copy_pair_xT(c):
                act.wait_ge(pair_xT_psum, c + 1)
                a.activation(xT[:].rearrange("p t c -> p (t c)"), bank[6][:], ACT.Copy).then_inc(pair_xT, 1)

            def copy_pair_proj(c, src):
                act.wait_ge(pair_proj_psum, c + 1)
                both = src[:, 0:2 * (2 * HS + E)].rearrange("p (t c) -> p t c", t=2)
                a.activation(en[:], both[:, :, 2 * HS:], ACT.Exp, scale=-1.0).then_inc(pair_proj, 1)
                a.activation(tg[:], both[:, :, HS:2 * HS], ACT.Tanh, scale=0.5).then_inc(pair_proj, 1)
                a.activation(pj[:], both, ACT.Copy).then_inc(pair_proj, 1)

            def copy_pair_shT(c, src):
                act.wait_ge(pair_slot_psum, c + 1)
                a.activation(shT[:], src[0:HS, P:3 * P].rearrange("p (t c) -> p t c", t=2), ACT.Copy).then_inc(pair_shT, 1)

            def copy_pt(U, n):
                act.wait_ge(pt_psum, U + 1)
                need(act, pv_done, U - 1)
                a.activation(PT[n % 2][:], bank[2 + n % 2][:], ACT.Copy).then_inc(pt_ready, 1)

            def copy_o(b, t):
                act.wait_ge(pv_done, UNITS * b + UNITS - 2 + 2 * t)
                a.activation(OT[:, t, :], bank[4 + t][:], ACT.Copy).then_inc(OT_ready, 1)

            def body(b, u, first=False, last=False, pair=True, first_pair=False):
                for n in range(UNITS):
                    if n == 2 and not first:
                        copy_o(b - 1, 1)
                    if n == 2:
                        act.wait_ge(rel_ready, b + 1)
                        a.activation(wm[:, 0:MEM], rel[:], ACT.Exp, bias=wsc[:, 0:1], accum_out=wsc[:, 1:2])\
                         .then_inc(wm_ready, 1)
                    exps(b, u, n)
                    if n or not first:
                        copy_pt(UNITS * b + n - 1, (n - 1) % UNITS)
                    if n == 0 and not first:
                        copy_o(b - 1, 0)
                    if n == 1 and not last:
                        copy_xT2(b + 1)
                    if n == 2 and not last:
                        copy_qT(b + 1, 1 - u)
                    if n == 3 and pair:
                        copy_pair_xT(b - 2)
                    if n == 4 and pair:
                        copy_pair_proj(b - 2, bank[7])
                    if n == 3 and not first:
                        act.wait_ge(mixT_psum, b)
                        a.activation(mixT[:].rearrange("p c t -> p (c t)"), bank[7][:], ACT.Copy).then_inc(mixT_ready, 1)
                    if n == 4 and not last:
                        copy_kT(b + 1)
                    if n == 6 and not last:
                        copy_v(b + 1, 1 - u)
                    if n == 10 and pair:
                        copy_pair_shT(b - 2, bank[7])

            def attention_():
                act.wait_ge(aw_loaded, 112)
                a.activation(gt[:, 1:2], gt[:, 0:1], ACT.Exp, scale=-1.0).then_inc(gate_exp, 1)
                copy_xT2(0)
                copy_qT(0, 0)
                copy_kT(0)
                copy_v(0, 0)
                body(0, 0, first=True, pair=False)
                body(1, 1, pair=False)
                body(2, 0, first_pair=True)
                with act.Fori(1, B // 2 - 1) as i:
                    body(2 * i + 1, 1)
                    body(2 * i + 2, 0)
                body(B - 1, 1, last=True)
                copy_pt(UNITS * B - 1, UNITS - 1)
                c = EARLY // 2 - 1
                copy_o(B - 1, 0)
                copy_pair_xT(c)
                copy_o(B - 1, 1)
                copy_pair_proj(c, bank[2])
                act.wait_ge(mixT_psum, B)
                a.activation(mixT[:].rearrange("p c t -> p (c t)"), bank[7][:], ACT.Copy).then_inc(mixT_ready, 1)
                copy_pair_shT(c, bank[3])

            for f in range(LAYERS):
                moe(f)
                if f == 0:
                    attention_()

        @block.vector
        def _(dve):
            v = nc.vector
            own = Own(dve, dve_own)

            def stats(t):
                own.mark(v.bn_stats(st[:, t, :], X[:, t, :]))

            def variance(t0=0, t1=NT):
                t = slice(t0, t1) if isinstance(t0, int) else bass.ds(t0, 2)
                own.settle()
                own.mark(v.tensor_tensor(mean[:, t], st[:, t, 1], st[:, t, 4], ALU.add))
                own.mark(v.tensor_tensor(dev[:, t], st[:, t, 1], st[:, t, 4], ALU.subtract))
                own.link(v.tensor_tensor(ve[:, t], st[:, t, 2], st[:, t, 5], ALU.add))
                own.mark(v.tensor_scalar(mean[:, t], mean[:, t], 0.5, None, ALU.mult))
                own.mark(v.tensor_scalar(ve[:, t], ve[:, t], 1.0 / C, LN_EPS, ALU.mult, ALU.add))
                own.link(v.scalar_tensor_tensor(dev[:, t], dev[:, t], 0.25, dev[:, t], ALU.mult, ALU.mult))
                v.tensor_tensor(ve[:, t], ve[:, t], dev[:, t], ALU.add).then_inc(var_ready, 1)

            def normalise2(b):
                for t in range(2):
                    last = v.tensor_scalar(xn[:, t, :], X[:, 2 * b + t, :], mean[:, bass.ds(2 * b + t, 1)],
                                           rstd[:, bass.ds(2 * b + t, 1)], ALU.subtract, ALU.mult)
                    last.then_inc(xn2_ready, 1)

            own.mark(v.memset(sg[:, 0, E:], -1.0))
            own.mark(v.memset(sg[:, 1, E:], -1.0))
            dve.wait_ge(const_set, 10)
            dve.wait_ge(x_loaded, 16)
            with own.loop(0, NT, 1) as t:
                stats(t)
            variance()

            def moe(f):
                dve.wait_ge(rstd_ready, (2 + B) * f + 1)

                if not f:
                    v.tensor_copy(chosen[:], expert_no[:]).then_inc(chosen_ready, 1)

                def normalise(i, u):
                    t = 2 * i + u
                    if f or not (isinstance(i, int) and i == 0):
                        dve.wait_ge(xT_psum, t + SHIFT * f - 1)
                        dve.wait_ge(row_ready, t + SHIFT * f - 1)
                    v.tensor_scalar(xn[:, u, :], X[:, bass.ds(t, 1), :].rearrange("p o c -> p (o c)"), mean[:, bass.ds(t, 1)],
                                    rstd[:, bass.ds(t, 1)], ALU.subtract, ALU.mult).then_inc(xn_ready, 1)

                def route(i, u):
                    s = 2 * i + u + SHIFT * f
                    proj = bank[2 + u]
                    dve.wait_ge(e_ready, s + 1)
                    own.link(v.tensor_scalar_add(sg[:, u, 0:E], en[:, u, :], 1.0))
                    own.link(v.reciprocal(sg[:, u, 0:E], sg[:, u, 0:E]))
                    dve.wait_ge(tg_ready, s + 1)
                    own.mark(v.scalar_tensor_tensor(sh1[:], tg[:, u, :], 1.0, proj[:, HS:2 * HS], ALU.add, ALU.mult))
                    own.link(v.max(top8[:], sg[:, u, 0:E]))
                    v.tensor_tensor(sh[:, u, :], proj[:, 0:HS], sh1[:], ALU.mult).then_inc(sh_ready, 1)
                    own.mark(v.reduce_sum(ssum[:, 0:1], top8[:, 0:TOPK], AX.X))
                    own.link(v.memset(top8[:, TOPK:8], -1.0))
                    own.mark(v.reciprocal(ssum[:, 1:2], ssum[:, 0:1]))
                    own.link(v.match_replace(rep[:], top8[:], sg[:, u, :], -1.0))
                    v.tensor_tensor(mask[:, u, :], rep[:, 0:E], sg[:, u, 0:E], ALU.is_lt).then_inc(mask_ready, 1)
                    own.link(v.tensor_scalar(ssum[:, 2:3], ssum[:, 1:2], 0.25, None, ALU.mult))
                    dve.wait_ge(mask_ready, s + 1)
                    own.mark(v.tensor_tensor(end_of[:, u, :], slot_end[:], mask[:, u, :], ALU.mult))
                    v.scalar_tensor_tensor(rows[:, bass.ds(2 * i + u, 1), C:C + E].rearrange("p o c -> p (o c)"),
                                           sg[:, u, 0:E], ssum[:, 2:3], mask[:, u, :],
                                           ALU.mult, ALU.mult).then_inc(weights_ready, 1)

                def place(i, u):
                    t = 2 * i + u
                    s = t + SHIFT * f
                    at = bank[4][:, 0:E]
                    dve.wait_ge(slot_psum, s + 1)
                    own.link(v.tensor_tensor(fits[:], at, end_of[:, u, :], ALU.is_lt))
                    own.link(v.scalar_tensor_tensor(key[:], at, 1.0, fits[:], ALU.add, ALU.mult))
                    v.tensor_tensor(chosen[:], chosen[:], mask[:, u, :], ALU.add).then_inc(chosen_ready, 1)
                    own.link(v.max(key8[:], key[:]))
                    own.link(v.scalar_tensor_tensor(over[:], key8[:, 0:TOPK], 0.0, over_row[:, bass.ds(TOPK * t, TOPK)],
                                                    ALU.is_equal, ALU.mult))
                    v.scalar_tensor_tensor(slot[:, bass.ds(t, 1), :].rearrange("p o k -> p (o k)"), key8[:, 0:TOPK], -1.0,
                                           over[:], ALU.add, ALU.add).then_inc(slot_ready, 1)

                def add_shared(i, u):
                    t = 2 * i + u
                    x = X[:, bass.ds(t, 1), :].rearrange("p o c -> p (o c)")
                    dve.wait_ge(shd_psum, t + SHIFT * f + 1)
                    v.scalar_tensor_tensor(x, bank[6 + u][:, 0:C], 0.25, x, ALU.mult, ALU.add)\
                     .then_inc(x_shared, 1)

                i0 = FIRST[f] // 2
                normalise(i0, 0)
                normalise(i0, 1)
                route(i0, 0)
                if i0 < HALF - 1:
                    with own.loop(i0, HALF - 1, 28) as i:
                        normalise(i + 1, 0)
                        route(i, 1)
                        place(i, 0)
                        add_shared(i, 0)
                        normalise(i + 1, 1)
                        route(i + 1, 0)
                        place(i, 1)
                        add_shared(i, 1)
                route(HALF - 1, 1)
                place(HALF - 1, 0)
                add_shared(HALF - 1, 0)
                place(HALF - 1, 1)
                add_shared(HALF - 1, 1)

                def copy_xd(i, u):
                    dve.wait_ge(t1_psum, 2 * i + u + NG * f + 1)
                    v.tensor_copy(xdT[u][:, 1, :], bank[1][:]).then_inc(xd1_ready, 1)

                def hidden(i, u):
                    gi = 2 * i + u
                    dve.wait_ge(meta_ready, gi + NG * f + 1)
                    v.tensor_copy(IDX[:, bass.ds(EG * gi, EG)], meta[u][:, :, META - 1]).then_inc(idx_ready, 1)
                    up = bank[2 + u][:, 0:EG * 2 * H].rearrange("p (e h) -> p e h", e=EG)
                    dve.wait_ge(eg_ready, gi + NG * f + 1)
                    own.link(v.scalar_tensor_tensor(eg[u][:], eg[u][:], 1.0, up[:, :, 0:H], ALU.add, ALU.mult))
                    for e in range(EG):
                        last = v.scalar_tensor_tensor(hbig[u][:, e * P + e * H:e * P + e * H + H], eg[u][:, e, :],
                                                      meta[u][:, e, bass.ds(EG * gi + e, 1)], up[:, e, H:],
                                                      ALU.mult, ALU.mult)
                        if e < EG - 1:
                            own.mark(last)
                    last.then_inc(h_ready, 1)

                def copy_y(i, u):
                    dve.wait_ge(y_psum, 2 * i + u + NG * f + 1)
                    if not (isinstance(i, int) and i == 0):
                        dve.wait_ge(acc_done[2], i * 32 + (16 * u - 16 + ADDS * f))
                        dve.wait_ge(acc_done[3], i * 32 + (16 * u - 16 + ADDS * f))
                    v.tensor_copy(ysb[u][:, 2:4, :], bank[6][:].rearrange("p (e c) -> p e c", e=2)).then_inc(yb_ready, 1)

                def estep(i, u, rows_=True, ups=True):
                    if rows_:
                        copy_xd(i + 1 + u, 1 - u)
                    if ups:
                        hidden(i + 1, u)
                    copy_y(i, u)

                copy_xd(0, 0)
                copy_xd(0, 1)
                hidden(0, 0)
                copy_xd(1, 0)
                hidden(0, 1)
                estep(0, 0)
                estep(0, 1)
                estep(1, 0)
                with own.loop(1, NG // 2 - 2, 8) as i:
                    estep(i, 1)
                    estep(i + 1, 0)
                estep(NG // 2 - 2, 1, rows_=False)
                estep(NG // 2 - 1, 0, rows_=False, ups=False)
                estep(NG // 2 - 1, 1, rows_=False, ups=False)

                for c, (t0, t1) in enumerate(PARTS):
                    dve.wait_ge(fin_loaded[c], 16 * ACCS * (f + 1))
                    own.mark(v.tensor_tensor(X[:, t0:t1, :], X[:, t0:t1, :], fin[:, t0:t1, :], ALU.add))
                    f2, f3 = (m[c % 2][:, 0:t1 - t0, :] for m in (fin2, fin3))
                    own.link(v.tensor_tensor(f2, f2, f3, ALU.add))
                    v.tensor_tensor(X[:, t0:t1, :], X[:, t0:t1, :], f2, ALU.add).then_inc(summed, 1)
                    if f + 1 < LAYERS:
                        own.settle()
                        dve.wait_ge(summed, len(PARTS) * f + c + 1)
                        for t in range(t0, t1):
                            stats(t)
                        if c == 0:
                            variance(t0, t1)
                            dve.wait_ge(rstd_ready, 2)
                            normalise2(0)
                if f + 1 < LAYERS:
                    variance(PARTS[0][1], NT)

            def rowmax(b, n):
                U = UNITS * b + n
                k = 4 if n % 3 == 0 else 2
                dve.wait_ge(s_psum, U + 1)
                v.tensor_reduce(negmax[n % 2][:, 0:k], bank[n % 2][:].rearrange("p (h t) -> p h t", h=k), AX.X, ALU.max,
                                negate=True).then_inc(max_ready, 1)

            def sigmas(b, u):
                flat = sigma[u][:].rearrange("p c t -> p (c t)")
                dve.wait_ge(expq_ready, b + 1)
                own.link(v.tensor_scalar(flat, flat, 1.0, None, ALU.min))
                v.scalar_tensor_tensor(flat, qT[:], 0.0, flat, ALU.max, ALU.add).then_inc(sigma_ready, 1)

            def raws(b):
                dve.wait_ge(raw_psum, b + 1)
                v.tensor_copy(raw[:].rearrange("p t m -> p (t m)"), bank[6][:, 0:2 * MEM]).then_inc(raw_ready, 1)

            def rels(b):
                dve.wait_ge(rel_psum, b + 1)
                own.link(v.tensor_copy(rel[:], bank[6][:, 16:16 + MEM]))
                v.tensor_reduce(wsc[:, 0:1], rel[:], AX.X, ALU.max, negate=True).then_inc(rel_ready, 1)

            def coefs(b):
                own.link(v.tensor_scalar(rawc[:], raw[:], CLIP, None, ALU.max))
                own.link(v.reciprocal(rawc[:], rawc[:]))
                dve.wait_ge(wm_ready, b + 1)
                own.link(v.reciprocal(wsc[:, 2:3], wsc[:, 1:2]))
                own.link(v.tensor_scalar(wm[:, MEM:], wm[:, 0:MEM], wsc[:, 2:3], gt[:, 2:3], ALU.mult, ALU.mult))
                for t in range(2):
                    own.mark(v.tensor_tensor(coef[:, t, :], rawc[:, t, :], wm[:, MEM:], ALU.mult))

            def mem_sum(b, j):
                t, half = j // 2, j % 2
                if j == 0:
                    own.settle()
                dve.wait_ge(mem_psum, 4 * b + j + 1)
                pm = bank[6]
                for k in range(2):
                    src, c = pm[:, C * k:C * k + C], coef[:, t, 2 * half + k:2 * half + k + 1]
                    if half == 0 and k == 0:
                        own.link(v.tensor_scalar(memo[:, t, :], src, c, None, ALU.mult))
                    elif k == 0:
                        own.link(v.scalar_tensor_tensor(memo[:, t, :], src, c, memo[:, t, :], ALU.mult, ALU.add))
                    else:
                        v.scalar_tensor_tensor(memo[:, t, :], src, c, memo[:, t, :], ALU.mult, ALU.add)\
                         .then_inc(mem_used, 1)
                        if half == 0:
                            dve.wait_ge(mem_used, 4 * b + j + 1)

            def finalise(b, t):
                dve.wait_ge(o_turned, 2 * b + t + 1)
                o = bank[4 + t][:].rearrange("p (h d) -> p h d", h=NHEAD)
                own.link(v.reciprocal(rl[:, t, :], o[:, :, HD]))
                own.link(v.tensor_scalar(rl[:, t, :], rl[:, t, :], gt[:, 3:4], None, ALU.mult))
                w = rl[:, t, :].rearrange("p (h o) -> p h o", o=1).to_broadcast([P, NHEAD, HD])
                v.tensor_tensor(mix[:, t, :].rearrange("p (h d) -> p h d", h=NHEAD), o[:, :, 0:HD], w, ALU.mult)\
                 .then_inc(o_used, 1)
                if t == 1:
                    dve.wait_ge(o_used, 2 * b + 2)
                    dve.wait_ge(mem_used, 4 * b + 4)
                    v.tensor_tensor(mix[:], mix[:], memo[:], ALU.add).then_inc(mix_ready, 1)

            def pair_normalise(c, u):
                dve.wait_ge(rstd_ready, c + 4)
                dve.wait_ge(pair_ids, c + 1)
                for t in range(2):
                    v.tensor_scalar(rowp[u][:, t, 0:C], X[:, bass.ds(2 * c + t, 1), :].rearrange("p o c -> p (o c)"),
                                    mean[:, bass.ds(2 * c + t, 1)], rstd[:, bass.ds(2 * c + t, 1)],
                                    ALU.subtract, ALU.mult).then_inc(pair_xn, 1)

            def pair_route(c, u, step):
                if step == 0:
                    dve.wait_ge(pair_proj, 3 * c + 3)
                    own.link(v.tensor_scalar_add(sg[:, :, 0:E], en[:], 1.0))
                    own.mark(v.reciprocal(sg[:, :, 0:E], sg[:, :, 0:E]))
                    own.mark(v.scalar_tensor_tensor(sh1p[:], tg[:], 1.0, pj[:, :, HS:2 * HS], ALU.add, ALU.mult))
                if step == 1:
                    own.settle()
                    v.tensor_tensor(sh[:], pj[:, :, 0:HS], sh1p[:], ALU.mult).then_inc(pair_sh, 1)
                    own.mark(v.max(top8p[:, 0, :], sg[:, 0, 0:E]))
                    own.link(v.max(top8p[:, 1, :], sg[:, 1, 0:E]))
                    own.mark(v.reduce_sum(ssump[:, 0, :], top8p[:, :, 0:TOPK], AX.X))
                    own.link(v.memset(top8p[:, :, TOPK:8], -1.0))
                if step == 2:
                    own.mark(v.reciprocal(ssump[:, 1, :], ssump[:, 0, :]))
                    own.mark(v.match_replace(repp[:, 0, :], top8p[:, 0, :], sg[:, 0, :], -1.0))
                    own.link(v.match_replace(repp[:, 1, :], top8p[:, 1, :], sg[:, 1, :], -1.0))
                    v.tensor_tensor(mask[:], repp[:, :, 0:E], sg[:, :, 0:E], ALU.is_lt).then_inc(pair_mask, 1)
                    own.mark(v.tensor_scalar(ssump[:, 2, :], ssump[:, 1, :], 0.25, None, ALU.mult))
                if step == 3:
                    own.settle()
                    dve.wait_ge(pair_mask, c + 1)
                    ends = slot_end[:].rearrange("p (o e) -> p o e", o=1).to_broadcast([P, 2, E])
                    own.mark(v.tensor_tensor(end_of[:], ends, mask[:], ALU.mult))
                    for t in range(2):
                        v.scalar_tensor_tensor(rowp[u][:, t, C:C + E], sg[:, t, 0:E], ssump[:, 2, t:t + 1], mask[:, t, :],
                                               ALU.mult, ALU.mult).then_inc(pair_weights, 1)

            def pair_place(c, src):
                at = src[:, 0:2 * E].rearrange("p (t e) -> p t e", t=2)
                dve.wait_ge(pair_slot_psum, c + 1)
                dve.wait_ge(pair_shT, c + 1)
                own.link(v.tensor_tensor(fitsp[:], at, end_of[:], ALU.is_lt))
                v.scalar_tensor_tensor(keyp[:], at, 1.0, fitsp[:], ALU.add, ALU.mult).then_inc(pair_slot_used, 1)
                own.link(v.tensor_tensor(chosen[:], chosen[:], mask[:, 0, :], ALU.add))
                dve.wait_ge(pair_slot_used, c + 1)
                v.tensor_tensor(chosen[:], chosen[:], mask[:, 1, :], ALU.add).then_inc(chosen_ready, 1)
                own.mark(v.max(key8p[:, 0, :], keyp[:, 0, :]))
                own.link(v.max(key8p[:, 1, :], keyp[:, 1, :]))
                at_row = over_row[:, bass.ds(2 * TOPK * c, 2 * TOPK)].rearrange("p (t k) -> p t k", t=2)
                own.link(v.scalar_tensor_tensor(overp[:], key8p[:, :, 0:TOPK], 0.0, at_row, ALU.is_equal, ALU.mult))
                v.scalar_tensor_tensor(slot[:, bass.ds(2 * c, 2), :], key8p[:, :, 0:TOPK], -1.0, overp[:],
                                       ALU.add, ALU.add).then_inc(pair_slot, 1)

            def pair_add(c, src):
                x2 = X[:, bass.ds(2 * c, 2), :]
                dve.wait_ge(pair_shd_psum, c + 1)
                v.scalar_tensor_tensor(x2, src[:].rearrange("p (t c) -> p t c", t=2), 0.25, x2, ALU.mult, ALU.add)\
                 .then_inc(pair_added, 1)

            def residual(b):
                dve.wait_ge(wo_psum, b + 1)
                x2 = X[:, bass.ds(2 * b, 2), :]
                v.tensor_tensor(x2, x2, bank[7][:].rearrange("p (t c) -> p t c", t=2), ALU.add).then_inc(wo_used, 1)
                dve.wait_ge(wo_used, b + 1)
                stats(2 * b)
                stats(2 * b + 1)

            def body(b, u, first=False, last=False, pair=True, first_pair=False):
                for n in range(UNITS):
                    U = UNITS * b + n
                    rowmax(b, n)
                    if n == 0:
                        raws(b)
                        if not last:
                            normalise2(b + 1)
                    if n == 1:
                        rels(b)
                    if n in (1, 2) and not first:
                        finalise(b - 1, n - 1)
                    if n == 3 and not last:
                        sigmas(b + 1, 1 - u)
                    if n == 4:
                        coefs(b)
                    if n == 5 and not first:
                        residual(b - 1)
                    if pair and n == 0 and not first_pair:
                        pair_add(b - 3, bank[7])
                    if pair and n == 1:
                        pair_normalise(b - 2, u)
                    if pair and 6 <= n < 10:
                        pair_route(b - 2, u, n - 6)
                    if n == 10 and not first:
                        variance(2 * (b - 1), 2 * b)
                    if pair and n == 11:
                        pair_place(b - 2, bank[7])
                    if 7 <= n < 11:
                        mem_sum(b, n - 7)

            def attention_():
                dve.wait_ge(gate_exp, 1)
                own.link(v.tensor_scalar_add(gt[:, 1:2], gt[:, 1:2], 1.0))
                own.link(v.reciprocal(gt[:, 2:3], gt[:, 1:2]))
                own.link(v.tensor_scalar(gt[:, 3:4], gt[:, 2:3], -1.0, 1.0, ALU.mult, ALU.add))
                v.tensor_copy(chosen[:], expert_no[:]).then_inc(chosen_ready, 1)
                sigmas(0, 0)
                dve.wait_ge(rstd_ready, 3)
                body(0, 0, first=True, pair=False)
                body(1, 1, pair=False)
                body(2, 0, first_pair=True)
                with own.loop(1, B // 2 - 1, 2 * 41) as i:
                    body(2 * i + 1, 1)
                    body(2 * i + 2, 0)
                body(B - 1, 1, last=True)
                c = EARLY // 2 - 1
                pair_add(c - 1, bank[7])
                pair_normalise(c, c % 2)
                finalise(B - 1, 0)
                finalise(B - 1, 1)
                for step in range(4):
                    pair_route(c, c % 2, step)
                residual(B - 1)
                variance(2 * (B - 1), 2 * B)
                pair_place(c, bank[3])
                pair_add(c, bank[0])

            for f in range(LAYERS):
                moe(f)
                if f == 0:
                    attention_()

        @block.tensor
        def _(pe):
            m = nc.tensor
            pe.wait_ge(const_ready, 9)
            pe.wait_ge(tok_loaded, 32)

            def warm_up(count):
                for _ in range(count):
                    m.matmul(bank[0][:], identb[:], causal[:].rearrange("p h t -> p (h t)"), start=True, stop=True)


            def moe(f):
                def project(i, u):
                    s = 2 * i + u + SHIFT * f
                    pe.wait_ge(xn_ready, s + 1)
                    for c in range(CC):
                        last = m.transpose(bank[u][:, P * c:P * c + P], xn[:, u, P * c:P * c + P], ident[:])
                    last.then_inc(xT_psum, 1)
                    pe.wait_ge(xT_ready, s + 1)
                    for c in range(CC):
                        last = m.matmul(bank[2 + u][:, 0:2 * HS + E], xT[:, u, P * c:P * c + P], wtok[:, c, :],
                                        start=(c == 0), stop=(c == CC - 1))
                    last.then_inc(proj_ready, 1)

                def turn(i, u):
                    t = 2 * i + u
                    s = t + SHIFT * f
                    pe.wait_ge(sh_ready, s + 1)
                    pe.wait_ge(mask_ready, s + 1)
                    pe.wait_ge(chosen_ready, t + CHOSEN0[f])
                    m.matmul(bank[4][:, 0:E], ones[:], chosen[:], start=True, stop=False)
                    m.matmul(bank[4][:, 0:E], before[:], mask[:, u, :], start=False, stop=True)\
                     .then_inc(slot_psum, 1)
                    m.transpose(bank[5][0:HS, 0:P], sh[:, u, :], ident[:]).then_inc(shT_psum, 1)

                def shared_down(i, u):
                    s = 2 * i + u + SHIFT * f
                    pe.wait_ge(shT_ready, s + 1)
                    m.matmul(bank[6 + u][:, 0:C], shT[:, u, :], wsd[:], start=True, stop=True).then_inc(shd_psum, 1)

                i0 = FIRST[f] // 2
                project(i0, 0)
                project(i0, 1)
                turn(i0, 0)
                shared_down(i0, 0)
                if i0 < HALF - 1:
                    with pe.Fori(i0, HALF - 1) as i:
                        project(i + 1, 0)
                        turn(i, 1)
                        shared_down(i, 1)
                        project(i + 1, 1)
                        turn(i + 1, 0)
                        shared_down(i + 1, 0)
                turn(HALF - 1, 1)
                shared_down(HALF - 1, 1)

                def turn_rows(i, u):
                    gi = 2 * i + u
                    pe.wait_ge(slots_loaded[u], i * 16 + 16 * (NG // 2 * f + 1))
                    if f or not isinstance(i, int) or i > 0 or u > 0:
                        pe.wait_ge(xd0_ready, gi + NG * f)
                        pe.wait_ge(xd1_ready, gi + NG * f)
                    for c, sem_ in enumerate((t0_psum, t1_psum)):
                        for e in range(EG):
                            last = m.transpose(bank[c][:, P * e:P * e + P], xg[u][:, e, P * c:P * c + P], ident[:])
                        last.then_inc(sem_, 1)

                def up(i, u):
                    gi = 2 * i + u
                    pe.wait_ge(xd0_ready, gi + NG * f + 1)
                    pe.wait_ge(xd1_ready, gi + NG * f + 1)
                    for e in range(EG):
                        for c in range(CC):
                            last = m.matmul(bank[2 + u][:, 2 * H * e:2 * H * e + 2 * H], xdT[u][:, c, P * e:P * e + P],
                                            wup[:, c, EG * gi + e, :], start=(c == 0), stop=(c == CC - 1))
                    last.then_inc(up_psum, 1)

                def turn_hidden(i, u):
                    pe.wait_ge(h_ready, 2 * i + u + NG * f + 1)
                    for e in range(EG):
                        last = m.transpose(bank[4][:, P * e:P * e + P], hbig[u][:, P * e:P * e + P], ident[:])
                    last.then_inc(hT_psum, 1)

                def down(i, u):
                    gi = 2 * i + u
                    pe.wait_ge(hT_ready, gi + NG * f + 1)
                    if f or not isinstance(i, int) or i > 0 or u > 0:
                        pe.wait_ge(ya_ready, gi + NG * f)
                        pe.wait_ge(yb_ready, gi + NG * f)
                    for e in range(EG):
                        last = m.matmul(bank[5 + e // 2][:, C * (e % 2):C * (e % 2) + C], hT[u][:, P * e:P * e + P],
                                        wdn[:, gi, :], start=True, stop=True)
                    last.then_inc(y_psum, 1)

                def estep(i, u, rows_=True, ups=True):
                    if rows_:
                        turn_rows(i + 1 + u, 1 - u)
                    turn_hidden(i, u)
                    if ups:
                        up(i + 1, u)
                    down(i, u)

                pe.wait_ge(dispatched, 16 * TOPK * NT * (f + 1))
                warm_up(10)
                pe.wait_ge(w_loaded, 48)
                turn_rows(0, 0)
                turn_rows(0, 1)
                up(0, 0)
                turn_rows(1, 0)
                up(0, 1)
                estep(0, 0)
                with pe.Fori(0, NG // 2 - 2) as i:
                    estep(i, 1)
                    estep(i + 1, 0)
                estep(NG // 2 - 2, 1, rows_=False)
                estep(NG // 2 - 1, 0, rows_=False, ups=False)
                estep(NG // 2 - 1, 1, rows_=False, ups=False)

            def scores(b, u, n):
                U = UNITS * b + n
                if n == 0:
                    pe.wait_ge(stacked[u], (b - u + 2) * (8 * 2 * len(Q_SLOTS)))
                need(pe, p_ready, U - 1)
                hg, j = n // 3, n % 3
                out_, heads = bank[n % 2], range(4 * hg, 4 * hg + 4) if j == 0 else range(4 * hg + 2 * j - 2, 4 * hg + 2 * j)
                q0, w = (0, P) if j == 0 else (P, T)
                for i, h in enumerate(heads):
                    m.matmul(out_[:, w * i:w * i + w], QS[u][:, h, q0:q0 + P], KS[u][:, h, 0:w],
                             start=(i == 0), stop=False, skip_group_check=True)
                diag = out_[:].rearrange("p (h t) -> p h t", t=w)[:, :, w - P:w]
                m.matmul(diag, identb[:], causal[:, 0:len(heads), :], start=False, stop=True,
                         skip_group_check=True).then_inc(s_psum, 1)

            def turn_p(U, n):
                pe.wait_ge(p_ready, U + 1)
                need(pe, pt_ready, U - 1)
                for i in range(4):
                    last = m.transpose(bank[2 + n % 2][:, P * i:P * i + P], Pr[n % 2][:, P * i:P * i + P], ident[:])
                last.then_inc(pt_psum, 1)

            def values(b, u, n):
                U = UNITS * b + n
                pe.wait_ge(pt_ready, U + 1)
                if n == 0:
                    pe.wait_ge(v_ready, b + 1)
                if n < 2:
                    need(pe, o_used, 2 * b - 1 + n)
                hg, j = n // 3, n % 3
                for i in range(4):
                    h, t, kb = (4 * hg + i, 0, 0) if j == 0 else (4 * hg + 2 * j - 2 + i // 2, 1, i % 2)
                    last = m.matmul(bank[4 + t][QUAD * (h % 4):QUAD * (h % 4) + QUAD, P * (h // 4):P * (h // 4) + P],
                                    V[u][:, kb, h, :], PT[n % 2][:, P * i:P * i + P], start=(kb == 0), stop=(kb == t),
                                    tile_position=(0, QUAD * (h % 4)))
                last.then_inc(pv_done, 1)

            def turn_o(b, t):
                pe.wait_ge(OT_ready, 2 * b + t + 1)
                for j in range(4):
                    last = m.transpose(bank[4 + t][:, P * j:P * j + P], OT[:, t, P * j:P * j + P], ident[:])
                last.then_inc(o_turned, 1)

            LAST = EARLY // 2 - 1

            def last_pair(c):
                return isinstance(c, int) and c == LAST

            def pair_turn(c, u, last_batch):
                pe.wait_ge(pair_xn, 2 * c + 2)
                if last_pair(c):
                    pe.wait_ge(mem_used, 4 * B)
                elif last_batch:
                    pe.wait_ge(rel_ready, c + 3)
                else:
                    pe.wait_ge(q_ready, 2 * c + 8)
                for t in range(2):
                    for j in range(CC):
                        last = m.transpose(bank[6][:, C * t + P * j:C * t + P * j + P], rowp[u][:, t, P * j:P * j + P],
                                           ident[:])
                last.then_inc(pair_xT_psum, 1)

            def pair_project(c, b):
                out_ = bank[2] if last_pair(c) else bank[7]
                pe.wait_ge(pair_xT, c + 1)
                if last_pair(c):
                    pe.wait_ge(pt_ready, UNITS * B)
                else:
                    pe.wait_ge(mixT_ready, b)
                for t in range(2):
                    cols = slice((2 * HS + E) * t, (2 * HS + E) * (t + 1))
                    for j in range(CC):
                        last = m.matmul(out_[:, cols], xT[:, t, P * j:P * j + P], wtok[:, j, :],
                                        start=(j == 0), stop=(j == CC - 1))
                last.then_inc(pair_proj_psum, 1)

            def pair_places(c, b):
                out_ = bank[3] if last_pair(c) else bank[7]
                if not last_pair(c):
                    pe.wait_ge(wo_used, b)
                pe.wait_ge(pair_sh, c + 1)
                pe.wait_ge(pair_mask, c + 1)
                pe.wait_ge(chosen_ready, c + NT + 2)
                m.matmul(out_[:, 0:E], ones[:], chosen[:], start=True, stop=False)
                m.matmul(out_[:, 0:E], before[:], mask[:, 0, :], start=False, stop=True)
                m.matmul(out_[:, E:2 * E], ones[:], chosen[:], start=True, stop=False)
                m.matmul(out_[:, E:2 * E], ones[:], mask[:, 0, :], start=False, stop=False)
                m.matmul(out_[:, E:2 * E], before[:], mask[:, 1, :], start=False, stop=True)
                for t in range(2):
                    last = m.transpose(out_[0:HS, P * (t + 1):P * (t + 2)], sh[:, t, :], ident[:])
                last.then_inc(pair_slot_psum, 1)

            def pair_shared_down(c):
                out_ = bank[0] if last_pair(c) else bank[7]
                pe.wait_ge(pair_slot_used, c + 1)
                pe.wait_ge(pair_shT, c + 1)
                for t in range(2):
                    last = m.matmul(out_[:, C * t:C * t + C], shT[:, t, :], wsd[:], start=True, stop=True)
                last.then_inc(pair_shd_psum, 1)

            def turn_x(b):
                pe.wait_ge(xn2_ready, 2 * b + 2)
                need(pe, wo_used, b - 2)
                for c in range(CC):
                    for t in range(2):
                        last = m.transpose(bank[7][:, T * c + P * t:T * c + P * t + P], xn[:, t, P * c:P * c + P], ident[:])
                last.then_inc(xT2_psum, 1)

            def project_t(b, w, done):
                for d in range(CC):
                    for c in range(CC):
                        last = m.matmul(bank[6][:, T * d:T * d + T], w[:, c, P * d:P * d + P], xT2[:, c, :],
                                        start=(c == 0), stop=(c == CC - 1))
                last.then_inc(done, 1)

            def q_job(b):
                pe.wait_ge(xT2_ready, b + 1)
                need(pe, rel_ready, b)
                project_t(b, wq, q_psum)

            def k_job(b, pair=False):
                if pair:
                    pe.wait_ge(pair_xT, b - 2)
                pe.wait_ge(q_ready, 2 * b + 2)
                project_t(b, wk, k_psum)

            def v_job(b):
                pe.wait_ge(k_ready, 2 * b + 2)
                for t in range(2):
                    for c in range(CC):
                        last = m.matmul(bank[6][:, C * t:C * t + C], xT2[:, c, P * t:P * t + P], wv[:, c, :],
                                        start=(c == 0), stop=(c == CC - 1))
                last.then_inc(v_psum, 1)

            def raw_job(b, u):
                pe.wait_ge(sigma_ready, b + 1)
                need(pe, mem_used, 4 * b)
                if isinstance(b, int) and b == 0:
                    pe.wait_ge(v_ready, 1)
                for t in range(2):
                    for c in range(CC):
                        last = m.matmul(bank[6][:, MEM * t:MEM * t + MEM], sigma[u][:, c, P * t:P * t + P], nrm[:, c, :],
                                        start=(c == 0), stop=(c == CC - 1))
                last.then_inc(raw_psum, 1)

            def rel_job(b):
                pe.wait_ge(raw_ready, b + 1)
                for t in range(2):
                    last = m.matmul(bank[6][:, 16:16 + MEM], mean_w[:], raw[:, t, :], start=(t == 0), stop=(t == 1))
                last.then_inc(rel_psum, 1)

            def mem_job(b, u, j, last_batch):
                if j == 0:
                    pe.wait_ge(rel_ready, b + 1)
                    pe.wait_ge(v_ready, b + 1 if last_batch else b + 2)
                else:
                    pe.wait_ge(mem_used, 4 * b + j)
                for c in range(CC):
                    last = m.matmul(bank[6][:], sigma[u][:, c, P * (j // 2):P * (j // 2) + P],
                                    mems[:, c, 512 * (j % 2):512 * (j % 2) + 512], start=(c == 0), stop=(c == CC - 1))
                last.then_inc(mem_psum, 1)

            def mix_job(b, last_batch):
                pe.wait_ge(mix_ready, b + 1)
                if not last_batch:
                    pe.wait_ge(xT2_ready, b + 3)
                for c in range(CC):
                    for t in range(2):
                        last = m.transpose(bank[7][:, T * c + P * t:T * c + P * t + P], mix[:, t, P * c:P * c + P], ident[:])
                last.then_inc(mixT_psum, 1)

            def out_job(b, pair=False):
                pe.wait_ge(mixT_ready, b + 1)
                if pair:
                    pe.wait_ge(pair_proj, 3 * b)
                for t in range(2):
                    for c in range(CC):
                        last = m.matmul(bank[7][:, C * t:C * t + C], mixT[:, c, P * t:P * t + P], wo[:, c, :],
                                        start=(c == 0), stop=(c == CC - 1))
                last.then_inc(wo_psum, 1)

            def body(b, u, first=False, last=False, pair=True, first_pair=False):
                for n in range(UNITS):
                    U = UNITS * b + n
                    scores(b, u, n)
                    if n == 0:
                        raw_job(b, u)
                    if n == 1:
                        rel_job(b)
                    if n or not first:
                        turn_p(U - 1, (n - 1) % UNITS)
                    if n == 1 and not first:
                        turn_o(b - 1, 0)
                    if pair and n == 0 and not first_pair:
                        pair_shared_down(b - 3)
                    if pair and n == 1 and not first_pair:
                        pe.wait_ge(pair_added, b - 2)
                    if not last:
                        {1: turn_x, 2: q_job, 4: k_job, 6: v_job}.get(n, lambda b: None)(b + 1, *[pair] * (n == 4))
                    if n == 2 and not first:
                        turn_o(b - 1, 1)
                    if n == 3 and not first:
                        mix_job(b - 1, last)
                    if pair and n == 3:
                        pair_turn(b - 2, u, last)
                    if pair and n == 4:
                        pair_project(b - 2, b)
                    if pair and n == 10:
                        pair_places(b - 2, b)
                    if n == 5 and not first:
                        out_job(b - 1, pair)
                    if 7 <= n < 11:
                        mem_job(b, u, n - 7, last)
                    if n >= 2:
                        values(b, u, n - 2)
                    elif not first:
                        values(b - 1, 1 - u, n + UNITS - 2)

            def attention_():
                pe.wait_ge(aw_loaded, 112)
                turn_x(0)
                q_job(0)
                k_job(0)
                v_job(0)
                body(0, 0, first=True, pair=False)
                body(1, 1, pair=False)
                body(2, 0, first_pair=True)
                with pe.Fori(1, B // 2 - 1) as i:
                    body(2 * i + 1, 1)
                    body(2 * i + 2, 0)
                body(B - 1, 1, last=True)
                turn_p(UNITS * B - 1, UNITS - 1)
                pair_shared_down(LAST - 1)
                values(B - 1, 1, UNITS - 2)
                values(B - 1, 1, UNITS - 1)
                pair_turn(LAST, LAST % 2, True)
                turn_o(B - 1, 0)
                pair_project(LAST, B)
                turn_o(B - 1, 1)
                pe.wait_ge(pair_added, LAST)
                mix_job(B - 1, True)
                out_job(B - 1)
                pair_places(LAST, B)
                pair_shared_down(LAST)

            for f in range(LAYERS):
                moe(f)
                if f == 0:
                    attention_()


def kernel(L0_attn_x, L0_attn_w_q, L0_attn_w_k, L0_attn_w_v, L0_attn_w_o, L0_attn_gate, L0_attn_memories,
           L0_attn_memory_norms, L0_ffn_w_gate, L0_ffn_w_shared_up, L0_ffn_w_shared_down, L0_ffn_w_up, L0_ffn_w_down):
    import numpy as np
    import concourse.bacc as bacc
    from concourse.bass_utils import run_bass_kernel_spmd

    def chunked(w):
        return w.reshape(CC, P, -1).transpose(1, 0, 2)

    arrays = {
        "x": np.asarray(L0_attn_x).reshape(N, C),
        "w_tok": chunked(np.concatenate([np.asarray(L0_ffn_w_shared_up), np.asarray(L0_ffn_w_gate)], axis=1)),
        "w_shared_down": np.asarray(L0_ffn_w_shared_down),
        "w_up": np.asarray(L0_ffn_w_up).reshape(E, CC, P, 2 * H).transpose(2, 1, 0, 3),
        "w_down": np.asarray(L0_ffn_w_down).reshape(NG, P, C).transpose(1, 0, 2),
        "w_q": chunked(np.asarray(L0_attn_w_q).T),
        "w_k": chunked(np.asarray(L0_attn_w_k).T),
        "w_v": chunked(np.asarray(L0_attn_w_v).T),
        "w_o": chunked(np.asarray(L0_attn_w_o).T),
        "memories": chunked(np.asarray(L0_attn_memories).transpose(1, 0, 2).reshape(C, MEM * C)),
        "norms": chunked(np.asarray(L0_attn_memory_norms).T),
        "gate": np.asarray(L0_attn_gate).reshape(1, 1),
    }
    arrays = {k: np.ascontiguousarray(a) for k, a in arrays.items()}
    nc = bacc.Bacc("TRN2", target_bir_lowering=False, num_devices=1)
    args = [nc.dram_tensor(k, a.shape, F32, kind="ExternalInput").ap() for k, a in arrays.items()]
    out = nc.dram_tensor("out", (N, C), F32, kind="ExternalOutput").ap()
    table = nc.dram_tensor("table", (TABLE, ROW), F32, kind="Internal").ap()
    acc = [nc.dram_tensor(f"acc{r}", (DUMP, C), F32, kind="Internal").ap() for r in range(ACCS)]
    thirds = nc.dram_tensor("thirds", (2, 2, 3, C, T), BF16, kind="Internal").ap()
    program(nc, *args, thirds, out, table, acc)
    r = run_bass_kernel_spmd(nc, [arrays], core_ids=[0])
    return r.results[0]["out"].reshape(B, T, C)
```
